# Optimizing a Trainium2 kernel written in Bass

```python
import numpy as np
import jax
import jax.numpy as jnp

def _softmax(x, axis=-1):
    return jax.nn.softmax(x, axis=axis)

def _gelu(x):
    return jax.nn.gelu(x, approximate=True)

def _silu(x):
    return jax.nn.silu(x)

def _sigmoid(x):
    return jax.nn.sigmoid(x)

def _layernorm(x, axis=-1, eps=1e-05):
    m = jnp.mean(x, axis=axis, keepdims=True)
    v = jnp.var(x, axis=axis, keepdims=True)
    return (x - m) / jnp.sqrt(v + eps)

def _scatter_add(tgt, idx, src, axis=0):
    return tgt.at[idx].add(src)

def _segment_sum(src, seg, n):
    return jax.ops.segment_sum(src, seg, n)
kernel_name = 'mk_adj_resnorm_d2_adj_r2_ad8cc3'

def setup_inputs(seed: int=0):
    np.random.seed(seed)
    _w = jnp.asarray

    def _rec_inputs():
        import jax
        import jax.numpy as jnp
        _gk = jax.random.key(seed)
        x = -0.0005207 + 1.001 * jax.random.normal(jax.random.fold_in(_gk, 1), (32, 256, 256), jnp.float32)
        _a = jax.random.bernoulli(jax.random.fold_in(_gk, 2), 0.03125, (32, 256, 256))
        adj = _a
        return (x, adj)
    x, adj = _rec_inputs()

    def _L0_gnn_setup():
        import jax, jax.numpy as jnp
        import numpy as np
        EMB = 256
        HEADS = 8
        HEAD_DIM = 64
        INNER = HEADS * HEAD_DIM
        B, S = (2, 1024)
        SCALE = HEAD_DIM ** (-0.5)
        MIN_SCORE = -1000000000.0
        LN_EPS = 1e-05
        key = jax.random.key(seed)
        ks = jax.random.split(key, 6)
        x = jax.random.normal(ks[0], (B, S, EMB), dtype=jnp.float32)
        graph_mask = jax.random.uniform(ks[1], (B, S, S)) < 0.05
        gamma = jnp.ones((EMB,), jnp.float32)
        beta = jnp.zeros((EMB,), jnp.float32)
        w_qkv = jax.random.normal(ks[2], (3 * INNER, EMB), jnp.float32) * EMB ** (-0.5)
        w_out = jax.random.normal(ks[3], (EMB, INNER), jnp.float32) * INNER ** (-0.5)
        b_out = jnp.zeros((EMB,), jnp.float32)
        return {'x': x, 'graph_mask': graph_mask, 'gamma': gamma, 'beta': beta, 'w_qkv': w_qkv, 'w_out': w_out, 'b_out': b_out}
    _L0_gnn_all = _L0_gnn_setup()
    _L0_gnn_in = {k: v for k, v in _L0_gnn_all.items() if k in ('gamma', 'beta', 'w_qkv', 'w_out', 'b_out')}
    del _L0_gnn_all

    def _L1_gnn_setup():
        import jax, jax.numpy as jnp
        import numpy as np
        QUERY_DIM = 256
        HEADS = 4
        DIM_HEAD = 64
        INNER = HEADS * DIM_HEAD
        B, N = (4, 1024)
        key = jax.random.key(seed)
        ks = jax.random.split(key, 6)
        s = 1.0 / np.sqrt(QUERY_DIM)
        x = jax.random.normal(ks[0], (B, N, QUERY_DIM), dtype=jnp.float32)
        adjacency_mask = jax.random.randint(ks[1], (B, N, N), 0, 2) > 0
        Wq = jax.random.normal(ks[2], (QUERY_DIM, INNER), dtype=jnp.float32) * s
        Wk = jax.random.normal(ks[3], (QUERY_DIM, INNER), dtype=jnp.float32) * s
        Wv = jax.random.normal(ks[4], (QUERY_DIM, INNER), dtype=jnp.float32) * s
        Wo = jax.random.normal(ks[5], (INNER, QUERY_DIM), dtype=jnp.float32) * (1.0 / np.sqrt(INNER))
        bo = jnp.zeros((QUERY_DIM,), dtype=jnp.float32)
        return {'x': x, 'adjacency_mask': adjacency_mask, 'Wq': Wq, 'Wk': Wk, 'Wv': Wv, 'Wo': Wo, 'bo': bo}
    _L1_gnn_all = _L1_gnn_setup()
    _L1_gnn_in = {k: v for k, v in _L1_gnn_all.items() if k in ('Wq', 'Wk', 'Wv', 'Wo', 'bo')}
    del _L1_gnn_all
    return {'x': x, 'adj': adj, 'L0_gnn_gamma': _L0_gnn_in['gamma'], 'L0_gnn_beta': _L0_gnn_in['beta'], 'L0_gnn_w_qkv': _L0_gnn_in['w_qkv'], 'L0_gnn_w_out': _L0_gnn_in['w_out'], 'L0_gnn_b_out': _L0_gnn_in['b_out'], 'L1_gnn_Wq': _L1_gnn_in['Wq'], 'L1_gnn_Wk': _L1_gnn_in['Wk'], 'L1_gnn_Wv': _L1_gnn_in['Wv'], 'L1_gnn_Wo': _L1_gnn_in['Wo'], 'L1_gnn_bo': _L1_gnn_in['bo']}

def reference(x, adj, L0_gnn_gamma, L0_gnn_beta, L0_gnn_w_qkv, L0_gnn_w_out, L0_gnn_b_out, L1_gnn_Wq, L1_gnn_Wk, L1_gnn_Wv, L1_gnn_Wo, L1_gnn_bo):
    import jax
    import jax.numpy as jnp

    def _L0_gnn_ref(x, graph_mask, gamma, beta, w_qkv, w_out, b_out):
        import jax, jax.numpy as jnp
        import numpy as np
        EMB = 256
        HEADS = 8
        HEAD_DIM = 64
        INNER = HEADS * HEAD_DIM
        B, S = (2, 1024)
        SCALE = HEAD_DIM ** (-0.5)
        MIN_SCORE = -1000000000.0
        LN_EPS = 1e-05
        bsz, seq_len, _ = x.shape
        mu = jnp.mean(x, axis=-1, keepdims=True)
        var = jnp.mean(jnp.square(x - mu), axis=-1, keepdims=True)
        h = (x - mu) * jax.lax.rsqrt(var + LN_EPS) * gamma + beta
        qkv = h @ w_qkv.T
        q, k, v = jnp.split(qkv, 3, axis=-1)
        q = q.reshape(bsz, seq_len, HEADS, HEAD_DIM)
        k = k.reshape(bsz, seq_len, HEADS, HEAD_DIM)
        v = v.reshape(bsz, seq_len, HEADS, HEAD_DIM)
        scores = jnp.einsum('bihd,bjhd->bhij', q, k) * SCALE
        eye = jnp.eye(seq_len, dtype=bool)[None]
        mask = graph_mask | eye
        scores = jnp.where(mask[:, None], scores, MIN_SCORE)
        probs = jax.nn.softmax(scores, axis=-1)
        out = jnp.einsum('bhij,bjhd->bihd', probs, v)
        out = out.reshape(bsz, seq_len, INNER)
        return out @ w_out.T + b_out

    def _L1_gnn_ref(x, adjacency_mask, Wq, Wk, Wv, Wo, bo):
        import jax, jax.numpy as jnp
        import numpy as np
        QUERY_DIM = 256
        HEADS = 4
        DIM_HEAD = 64
        INNER = HEADS * DIM_HEAD
        B, N = (4, 1024)
        scale = DIM_HEAD ** (-0.5)

        def split_heads(t):
            b, n, _ = t.shape
            return t.reshape(b, n, HEADS, DIM_HEAD).transpose(0, 2, 1, 3)
        q = split_heads(x @ Wq)
        k = split_heads(x @ Wk)
        v = split_heads(x @ Wv)
        sim = jnp.einsum('bhid,bhjd->bhij', q, k) * scale
        neg = -jnp.finfo(sim.dtype).max
        sim = jnp.where(adjacency_mask[:, None, :, :], sim, neg)
        attn = jax.nn.softmax(sim, axis=-1)
        out = jnp.einsum('bhij,bhjd->bhid', attn, v)
        out = out.transpose(0, 2, 1, 3).reshape(x.shape[0], x.shape[1], INNER)
        return out @ Wo + bo
    x = _layernorm(x + _L0_gnn_ref(x, adj, L0_gnn_gamma, L0_gnn_beta, L0_gnn_w_qkv, L0_gnn_w_out, L0_gnn_b_out), axis=-1)
    x = _layernorm(x + _L1_gnn_ref(x, adj, L1_gnn_Wq, L1_gnn_Wk, L1_gnn_Wv, L1_gnn_Wo, L1_gnn_bo), axis=-1)
    return x

_drawn_inputs = setup_inputs


def setup_inputs(seed=0):
    import zlib

    import numpy as np

    out = dict(_drawn_inputs(seed))
    spreads = {'L0_gnn_gamma': (1.0, 0.2),
     'L0_gnn_beta': (0.0, 0.1),
     'L0_gnn_b_out': (0.0, 0.1),
     'L1_gnn_bo': (0.0, 0.1)}
    factors = {}
    for name, (base, spread) in spreads.items():
        noise = np.random.default_rng([zlib.crc32(name.encode()), seed]).standard_normal(out[name].shape)
        drawn = base * np.exp(spread * noise) if base else spread * noise
        out[name] = jnp.asarray(drawn.astype(out[name].dtype))
    for name, factor in factors.items():
        out[name] = (out[name] * factor).astype(out[name].dtype)
    return out
```

```python
from contextlib import ExitStack

import concourse.bass as bass
from concourse import mybir

F32 = mybir.dt.float32
F16 = mybir.dt.float16
U8 = mybir.dt.uint8
ALU = mybir.AluOpType
ACT = mybir.ActivationFunctionType

P = 128
GRAPHS, NODES, EMB = 32, 256, 256
HD = 64
NT = NODES // P
ET = EMB // P
VW = HD + 1
SCALE = HD ** -0.5
BIG = 3.0e38
WSCALE = 64.0
EPS = 1e-5
DMA = 16


class Graph:

    def __init__(self, i, t):
        self.n = 2 * i + t
        self.turn = i + t // 2
        self.par = t % 2
        self.live = not isinstance(self.n, int) or 0 <= self.n < GRAPHS


INPUT_T, QK, V, ATTN_T, OUT = "input_t", "qk", "v", "attn_t", "out"
SHIFT = {INPUT_T: 2, QK: 1, V: 1, ATTN_T: -1, OUT: -1}


class Chunk:

    def __init__(self, plan, i, u, slot):
        _, self.kind, self.index = plan[slot]
        self.graph = Graph(i, u + SHIFT[self.kind])
        j = 2 * i + u
        if isinstance(j, int):
            before = [kind for jj in range(-2, j + 1) for n, (_, kind, _) in enumerate(plan)
                      if (jj < j or n < slot) and 0 <= jj + SHIFT[kind] < GRAPHS]
            self.count, self.split = len(before), len(before) - before.count(OUT)
        else:
            first = Chunk(plan, 2, 0, slot)
            self.count = len(plan) * (j - 4) + first.count
            self.split = (len(plan) - 1) * (j - 4) + first.split
            assert len(plan) % 2 == 0
        self.bank = (self.count if isinstance(self.count, int) else first.count) % 2


def chunks(plan, i, u, step):
    found = [Chunk(plan, i, u, slot) for slot in range(len(plan)) if plan[slot][0] == step]
    return [c for c in found if c.graph.live]


def chunks_before(plan, heads, i, u, step):
    if step:
        return chunks(plan, i, u, step - 1)
    return chunks(plan, i, u - 1, heads - 1) if u else chunks(plan, i - 1, 1, heads - 1)


def read_count(plan, i, t, kind, index=0):
    slot = [(k, x) for _, k, x in plan].index((kind, index))
    t -= SHIFT[kind]
    return Chunk(plan, i + t // 2, t % 2, slot).count + 1


def due(count):
    return not isinstance(count, int) or count > 0


def over_graphs(eng, iteration):
    for j in range(-3, 4):
        iteration(j // 2, j % 2)
    with eng.Fori(2, GRAPHS // 2 - 2) as i:
        iteration(i, 0)
        iteration(i, 1)
    for j in range(GRAPHS - 4, GRAPHS + 2):
        iteration(j // 2, j % 2)


def build(nc, x, adj, gamma, beta, wqkv0, wo0, bo0, wq1, wk1, wv1, wo1, bo1, out):
    with ExitStack() as ctx:
        def sb(name, shape, dtype=F32):
            return ctx.enter_context(nc.sbuf_tensor(name, shape, dtype))

        def psum(name):
            return ctx.enter_context(nc.psum_tensor(name, [P, 512], F32))

        def sem(name):
            return ctx.enter_context(nc.semaphore(name))

        score_ps = [psum(f"score_ps{b}") for b in range(2)]
        probT_ps = [psum(f"probT_ps{b}") for b in range(2)]
        value_ps = [psum(f"value_ps{b}") for b in range(2)]
        work_ps = [psum(f"work_ps{b}") for b in range(2)]

        ident = sb("ident", [P, P])
        eps_t = sb("eps_t", [P, NT])
        minus_half = sb("minus_half", [P, NT])
        minus_one = sb("minus_one", [P, NT])
        gamma_b = sb("gamma_b", [P, EMB])
        beta_b = sb("beta_b", [P, EMB])
        mid = sb("mid", [P, GRAPHS, NT, EMB])
        x_in = [sb(f"x_in{b}", [P, NT, EMB]) for b in range(2)]
        x_res = [sb(f"x_res{b}", [P, NT, EMB]) for b in range(2)]
        adj_in = [sb(f"adj_in{b}", [P, NT, NODES], U8) for b in range(2)]
        mask = [sb(f"mask{b}", [P, NT, NODES]) for b in range(2)]
        normed = sb("normed", [P, NT, EMB])
        scaled = sb("scaled", [P, NT, EMB])
        h_in = [sb(f"h_in{b}", [P, NT, EMB]) for b in range(2)]
        hT_hi = sb("hT_hi", [P, ET, NODES], F16)
        hT_lo = sb("hT_lo", [P, ET, NODES], F16)
        qk_hi = sb("qk_hi", [P, 4, 2 * NODES], F16)
        qk_lo = sb("qk_lo", [P, 4, 2 * NODES], F16)
        qk_stack = [sb(f"qk_stack{b}", [P, 2, 4, 2 * NODES], F16) for b in range(2)]
        k_swap = [sb(f"k_swap{b}", [P, 2, 4, NODES], F16) for b in range(2)]
        v_hi = [sb(f"v_hi{b}", [P, NT, 8, VW], F16) for b in range(2)]
        v_lo = [sb(f"v_lo{b}", [P, NT, 8, HD], F16) for b in range(2)]
        low_max = sb("low_max", [P, 2, NT])
        prob = [sb(f"prob{b}", [P, NT, NODES]) for b in range(2)]
        probT_hi = [sb(f"probT_hi{b}", [P, NT, NODES], F16) for b in range(2)]
        probT_lo = [sb(f"probT_lo{b}", [P, NT, NODES], F16) for b in range(2)]
        inv_sum = sb("inv_sum", [P, 2, NT, 2])
        attn = [sb(f"attn{b}", [P, NT, 8 * HD]) for b in range(2)]
        attnT_hi = sb("attnT_hi", [P, NT, 4, P], F16)
        attnT_lo = sb("attnT_lo", [P, NT, 4, P], F16)
        y = [sb(f"y{b}", [P, NT, EMB]) for b in range(2)]
        y_out = [sb(f"y_out{b}", [P, NT, EMB]) for b in range(2)]

        class Stats:

            def __init__(self, name):
                self.parts = sb(f"{name}_parts", [P, NT, 6])
                self.mv = sb(f"{name}_mv", [P, NT, 2])
                self.vpe = sb(f"{name}_vpe", [P, NT])
                self.rstd = sb(f"{name}_rstd", [P, NT])
                self.mr = sb(f"{name}_mr", [P, NT])
                self.nmr = sb(f"{name}_nmr", [P, NT])

        class Norm:

            def __init__(self, name, stats):
                self.stats = stats
                self.bn_done = sem(f"{name}_bn_done")
                self.mv_done = sem(f"{name}_mv_done")
                self.vpe_done = sem(f"{name}_vpe_done")
                self.rstd_done = sem(f"{name}_rstd_done")
                self.mr_done = sem(f"{name}_mr_done")
                self.nmr_done = sem(f"{name}_nmr_done")

        class Layer:
            def __init__(self, name, heads, with_norm, eye, plan):
                self.heads, self.pairs, self.inner = heads, heads // 2, heads * HD
                self.with_norm, self.eye, self.plan = with_norm, eye, plan
                self.w_hi = sb(f"{name}_w_hi", [P, ET, 3 * self.inner], F16)
                self.w_lo = sb(f"{name}_w_lo", [P, ET, 3 * self.inner], F16)
                self.wo_hi = sb(f"{name}_wo_hi", [P, self.pairs, EMB], F16)
                self.wo_lo = sb(f"{name}_wo_lo", [P, self.pairs, EMB], F16)
                self.bias = sb(f"{name}_bias", [P, EMB])
                self.x_loaded = [sem(f"{name}_x_loaded{b}") for b in range(2)]
                self.adj_loaded = [sem(f"{name}_adj_loaded{b}") for b in range(2)]
                self.res_loaded = [sem(f"{name}_res_loaded{b}") for b in range(2)]
                self.stored = [sem(f"{name}_stored{b}") for b in range(2)]
                self.stacked = sem(f"{name}_stacked")
                self.x_norm = Norm(f"{name}_x", x_stats)
                self.x_normed = sem(f"{name}_x_normed")
                self.x_scaled = sem(f"{name}_x_scaled")
                self.h_ready = sem(f"{name}_h_ready")
                self.res_ready = sem(f"{name}_res_ready")
                self.mask_raw = sem(f"{name}_mask_raw")
                self.mask_ready = sem(f"{name}_mask_ready") if eye else self.mask_raw
                self.y_norm = Norm(f"{name}_y", y_stats)
                self.finished = sem(f"{name}_finished")
                self.work_done = sem(f"{name}_work_done")
                self.work_hi_done = sem(f"{name}_work_hi_done")
                self.work_read = sem(f"{name}_work_read")
                self.scores_done = sem(f"{name}_scores_done")
                self.masked = sem(f"{name}_masked")
                self.probs = sem(f"{name}_probs")
                self.probT_done = sem(f"{name}_probT_done")
                self.probT_hi_done = sem(f"{name}_probT_hi_done")
                self.probT_lo_done = sem(f"{name}_probT_lo_done")
                self.values_done = sem(f"{name}_values_done")
                self.inv_done = sem(f"{name}_inv_done")
                self.attn_done = sem(f"{name}_attn_done")

        x_stats, y_stats = Stats("x_stats"), Stats("y_stats")
        layer0 = Layer("l0", 8, True, True,
                       [(0, QK, 0), (1, QK, 1), (2, QK, 2), (2, ATTN_T, 0), (3, QK, 3), (3, ATTN_T, 1),
                        (4, V, 0), (5, V, 1), (6, OUT, 0), (7, INPUT_T, 0)])
        layer1 = Layer("l1", 4, False, False,
                       [(0, QK, 0), (1, QK, 1), (2, V, 0), (2, ATTN_T, 0), (3, OUT, 0), (3, INPUT_T, 0)])
        layers = (layer0, layer1)
        LOOKAHEAD = 3

        stage0 = mid[:, 0:6].rearrange("p g t e -> p (g t e)").rearrange("p (c n) -> p c n", c=ET)
        stage_o0 = mid[:, 6:8].rearrange("p g t e -> p (g t) e")
        stage1 = mid[:, 8:11].rearrange("p g t e -> p (g t e)").rearrange("p (c n) -> p c n", c=ET)
        stage_o1 = mid[:, 11:12].rearrange("p g t e -> p (g t) e")
        weights_loaded = sem("weights_loaded")
        biases_loaded = sem("biases_loaded")
        weights_hi = sem("weights_hi")
        weights_lo = sem("weights_lo")
        zeroed = sem("zeroed")
        constants = sem("constants")
        sp_passed, pool_passed, dve_passed = sem("sp_passed"), sem("pool_passed"), sem("dve_passed")
        splits = [(stage0, layer0.w_hi, layer0.w_lo), (stage_o0, layer0.wo_hi, layer0.wo_lo),
                  (stage1, layer1.w_hi, layer1.w_lo), (stage_o1, layer1.wo_hi, layer1.wo_lo)]
        WEIGHT_DMAS = 6

        def nodes_of(array, g):
            return array[bass.ds(g.n, 1)].rearrange("g (t p) c -> p (g t) c", p=P)

        def mid_of(g):
            return mid[:, bass.ds(g.n, 1)].rearrange("p g t e -> p (g t) e")

        def in_two(ps):
            return ps[:, :].rearrange("p (c n) -> p c n", c=2)

        def in_four(ps):
            return ps[:, :].rearrange("p (r n) -> p r n", n=P)

        def by_head(ps):
            return ps[:, :].rearrange("p (h d) -> p h d", d=HD)

        def v_dest(ly, tile, c):
            flat = tile[:, :, :, :].rearrange("p t h d -> p (t h) d")
            return flat[:, 8 * c:8 * c + 8, 0:HD]

        def v_head(ly, tile, kt, head, width):
            flat = tile[:, :, :, :].rearrange("p t h d -> p (t h) d")
            return flat[:, kt * ly.heads + head, 0:width]

        def attnT_dest(tile, c):
            flat = tile[:, :, :, :].rearrange("p t r n -> p (t r) n")
            return flat[:, 4 * c:4 * c + 4, :]

        def attnT_block(ly, tile, t, pair):
            flat = tile[:, :, :, :].rearrange("p t r n -> p (t r) n")
            return flat[:, t * ly.pairs + pair, :]

        FINISH_STEP, INPUT_NORM_STEP = 3, 4

        block = ctx.enter_context(nc.Block())

        @block.sync
        def _(sp):
            by_row = "(c p) n -> p c n"
            sp.dma_start(stage0, wqkv0.rearrange(by_row, p=P)).then_inc(weights_loaded, DMA)
            sp.dma_start(stage_o0, wo0.rearrange(by_row, p=P)).then_inc(weights_loaded, DMA)
            for n, w in enumerate((wq1, wk1, wv1)):
                sp.dma_start(stage1[:, :, n * layer1.inner:(n + 1) * layer1.inner],
                             w.rearrange(by_row, p=P)).then_inc(weights_loaded, DMA)
            sp.dma_start(stage_o1, wo1.rearrange(by_row, p=P)).then_inc(weights_loaded, DMA)
            for tile, row in ((gamma_b, gamma), (beta_b, beta), (layer0.bias, bo0), (layer1.bias, bo1)):
                sp.dma_start(tile[:, :], row.partition_broadcast(P)).then_inc(biases_loaded, DMA)

            def iteration(ly, i, u):
                g = Graph(i, u + LOOKAHEAD)
                if g.live:
                    if due(g.n - 1):
                        if ly.with_norm:
                            sp.wait_ge(ly.x_normed, g.n - 1)
                        else:
                            sp.wait_ge(ly.work_done, read_count(ly.plan, i, u + LOOKAHEAD - 2, INPUT_T))
                    src = nodes_of(x, g) if ly is layer0 else mid_of(g)
                    sp.dma_start(x_in[g.par][:, :, :], src).then_inc(ly.x_loaded[g.par], DMA)
                g = Graph(i, u + 2)
                if g.live:
                    if due(g.n - 1):
                        sp.wait_ge(ly.mask_raw, g.n - 1)
                        sp.sem_inc(sp_passed, 1)
                    sp.dma_start(adj_in[g.par][:, :, :], nodes_of(adj, g)).then_inc(ly.adj_loaded[g.par], DMA)
                g = Graph(i, u)
                if g.live:
                    if due(g.n - 1):
                        sp.wait_ge(ly.work_read, read_count(ly.plan, i, u - 2, OUT))
                    src = nodes_of(x, g) if ly is layer0 else mid_of(g)
                    sp.dma_start(x_res[g.par][:, :, :], src).then_inc(ly.res_loaded[g.par], DMA)
                g = Graph(i, u + 1)
                if g.live:
                    sp.wait_ge(ly.work_read, read_count(ly.plan, i, u + 1, QK, ly.pairs - 1))
                    sp.sem_inc(sp_passed, 1)
                    if due((g.n - 1) * ly.heads):
                        sp.wait_ge(ly.scores_done, (g.n - 1) * ly.heads)
                        sp.sem_inc(sp_passed, 1)
                    for half in range(2):
                        rows, all_pairs = slice(HD * half, HD * half + HD), slice(0, ly.pairs)
                        stack, swap = qk_stack[g.par][:, half, all_pairs, :], k_swap[g.par][:, half, all_pairs, :]
                        for dst, src in ((stack[0:HD], qk_hi[rows, all_pairs, :]),
                                         (stack[HD:P], qk_lo[rows, all_pairs, :]),
                                         (swap[0:HD], qk_lo[rows, all_pairs, NODES:2 * NODES]),
                                         (swap[HD:P], qk_hi[rows, all_pairs, NODES:2 * NODES])):
                            sp.dma_start(dst, src).then_inc(ly.stacked, DMA)
                g = Graph(i, u - 2)
                if g.live:
                    sp.wait_ge(ly.finished, g.n + 1)
                    dst = mid_of(g) if ly is layer0 else nodes_of(out, g)
                    sp.dma_start(dst, y_out[g.par][:, :, :]).then_inc(ly.stored[g.par], DMA)

            sp.wait_ge(weights_lo, len(splits))
            for ly in layers:
                over_graphs(sp, lambda i, u: iteration(ly, i, u))
                for b in range(2):
                    sp.wait_ge(ly.stored[b], DMA * GRAPHS // 2)

        @block.gpsimd
        def _(pool):
            nc.gpsimd.memset(ident[:, :], 0.0).then_inc(zeroed, 1)
            pool.wait_ge(zeroed, 1)
            nc.gpsimd.affine_select(out=ident[:, :], in_=ident[:, :], compare_op=ALU.not_equal, fill=1.0, base=0,
                                    pattern=[[-1, P]], channel_multiplier=1).then_inc(constants, 1)
            nc.gpsimd.memset(eps_t[:, :], EPS).then_inc(constants, 1)
            nc.gpsimd.memset(minus_half[:, :], -0.5).then_inc(constants, 1)
            nc.gpsimd.memset(minus_one[:, :], -1.0).then_inc(constants, 1)
            for b in range(2):
                nc.gpsimd.memset(v_hi[b][:, :, :, HD:VW], 1.0).then_inc(constants, 1)
            pool.wait_ge(constants, 6)
            pool.wait_ge(biases_loaded, 4 * DMA)

            def normaliser(norm, count):
                st = norm.stats
                nc.gpsimd.tensor_tensor(st.vpe[:, :], st.mv[:, :, 1], eps_t[:, :], ALU.add).then_inc(norm.vpe_done, 1)
                pool.wait_ge(norm.vpe_done, count)
                nc.gpsimd.tensor_tensor(st.rstd[:, :], st.vpe[:, :], minus_half[:, :],
                                        ALU.pow).then_inc(norm.rstd_done, 1)
                pool.wait_ge(norm.rstd_done, count)
                nc.gpsimd.tensor_tensor(st.mr[:, :], st.mv[:, :, 0], st.rstd[:, :],
                                        ALU.mult).then_inc(norm.mr_done, 1)
                pool.wait_ge(norm.mr_done, count)
                nc.gpsimd.tensor_tensor(st.nmr[:, :], st.mr[:, :], minus_one[:, :],
                                        ALU.mult).then_inc(norm.nmr_done, 1)

            def wide(row):
                return row[:, :].unsqueeze(1).broadcast_to([P, NT, EMB])

            def iteration(ly, i, u):
                g = Graph(i, u + 1)
                if g.live:
                    pool.wait_ge(ly.adj_loaded[g.par], DMA * (g.turn + 1))
                    if due((g.n - 1) * ly.heads):
                        pool.wait_ge(ly.masked, (g.n - 1) * ly.heads)
                    pool.sem_inc(pool_passed, 1)
                    nc.gpsimd.tensor_scalar(mask[g.par][:, :, :], adj_in[g.par][:, :, :], BIG, BIG,
                                            ALU.mult, ALU.subtract).then_inc(ly.mask_raw, 1)
                    if ly.eye:
                        pool.wait_ge(ly.mask_raw, g.n + 1)
                        pool.sem_inc(pool_passed, 1)
                        nc.gpsimd.affine_select(out=mask[g.par][:, :, :], in_=mask[g.par][:, :, :],
                                                compare_op=ALU.not_equal, fill=0.0, base=0,
                                                pattern=[[P, NT], [-1, NODES]],
                                                channel_multiplier=1).then_inc(ly.mask_ready, 1)
                g = Graph(i, u)
                if g.live:
                    pool.wait_ge(ly.res_loaded[g.par], DMA * (g.turn + 1))
                    nc.gpsimd.tensor_tensor(x_res[g.par][:, :, :], x_res[g.par][:, :, :], wide(ly.bias),
                                            ALU.add).then_inc(ly.res_ready, 1)
                g = Graph(i, u - 2)
                if g.live:
                    pool.wait_ge(ly.y_norm.mv_done, g.n + 1)
                    if due(g.n):
                        pool.wait_ge(ly.finished, g.n)
                    normaliser(ly.y_norm, g.n + 1)
                g = Graph(i, u + 2)
                if ly.with_norm and g.live:
                    pool.wait_ge(ly.x_norm.mv_done, g.n + 1)
                    if due(g.n):
                        pool.wait_ge(ly.x_normed, g.n)
                    normaliser(ly.x_norm, g.n + 1)
                    pool.wait_ge(ly.x_normed, g.n + 1)
                    nc.gpsimd.tensor_tensor(scaled[:, :, :], normed[:, :, :], wide(gamma_b),
                                            ALU.mult).then_inc(ly.x_scaled, 1)
                    pool.wait_ge(ly.x_scaled, g.n + 1)
                    if due(g.n - 1):
                        pool.wait_ge(ly.work_done, read_count(ly.plan, i, u, INPUT_T))
                    nc.gpsimd.tensor_tensor(h_in[g.par][:, :, :], scaled[:, :, :], wide(beta_b),
                                            ALU.add).then_inc(ly.h_ready, 1)

            for ly in layers:
                over_graphs(pool, lambda i, u: iteration(ly, i, u))
                for b in range(2):
                    pool.wait_ge(ly.stored[b], DMA * GRAPHS // 2)

        @block.scalar
        def _(act):
            act.wait_ge(weights_loaded, WEIGHT_DMAS * DMA)
            for stage, hi, _ in splits:
                nc.scalar.activation(hi[:, :, :], stage, ACT.Copy, scale=WSCALE).then_inc(weights_hi, 1)

            def high_part(ly, c):
                g, ps = c.graph, work_ps[c.bank]
                act.wait_ge(ly.work_done, c.count + 1)
                if c.kind == INPUT_T:
                    e = nc.scalar.activation(hT_hi[:, :, :], in_two(ps), ACT.Copy)
                elif c.kind == QK:
                    if c.index == 0 and due(g.n):
                        act.wait_ge(ly.stacked, 8 * DMA * g.n)
                    e = nc.scalar.activation(qk_hi[:, c.index, :], ps[:, :], ACT.Copy, scale=1 / WSCALE)
                elif c.kind == V:
                    if due((g.n - 1) * ly.heads):
                        act.wait_ge(ly.values_done, (g.n - 1) * ly.heads)
                    e = nc.scalar.activation(v_dest(ly, v_hi[g.par], c.index), by_head(ps), ACT.Copy,
                                             scale=1 / WSCALE)
                else:
                    e = nc.scalar.activation(attnT_dest(attnT_hi, c.index), in_four(ps), ACT.Copy)
                e.then_inc(ly.work_hi_done, 1)

            def iteration(ly, i, u):
                g, last, older, ahead = (Graph(i, u + t) for t in (0, -1, -2, 2))
                for h in range(ly.heads):
                    b = h % 2
                    for c in chunks_before(ly.plan, ly.heads, i, u, h):
                        if c.kind != OUT:
                            high_part(ly, c)
                    gt = g if h >= 1 else last
                    if gt.live:
                        n = g.n * ly.heads + h - 1
                        act.wait_ge(ly.probT_done, n + 1)
                        if due(n - 1):
                            act.wait_ge(ly.values_done, n - 1)
                        nc.scalar.activation(probT_hi[1 - b][:, :, :], in_two(probT_ps[1 - b]),
                                             ACT.Copy).then_inc(ly.probT_hi_done, 1)
                    if g.live:
                        n = g.n * ly.heads + h
                        act.wait_ge(ly.masked, n + 1)
                        if due(n - 1):
                            act.wait_ge(ly.probT_done, n - 1)
                        for qt in range(NT):
                            e = nc.scalar.activation(prob[b][:, qt, :],
                                                     score_ps[b][:, qt * NODES:(qt + 1) * NODES],
                                                     ACT.Exp, bias=low_max[:, b, qt:qt + 1], scale=-1.0)
                        e.then_inc(ly.probs, 1)
                    if h == FINISH_STEP and older.live:
                        act.wait_ge(ly.y_norm.nmr_done, older.n + 1)
                        if due(older.turn):
                            act.wait_ge(ly.stored[older.par], DMA * older.turn)
                        for t in range(NT):
                            e = nc.scalar.activation(y_out[older.par][:, t, :], y[older.par][:, t, :], ACT.Identity,
                                                     bias=y_stats.nmr[:, t:t + 1], scale=y_stats.rstd[:, t:t + 1])
                        e.then_inc(ly.finished, 1)
                    if h == INPUT_NORM_STEP and ly.with_norm and ahead.live:
                        act.wait_ge(ly.x_norm.nmr_done, ahead.n + 1)
                        if due(ahead.n):
                            act.wait_ge(ly.x_scaled, ahead.n)
                        for t in range(NT):
                            e = nc.scalar.activation(normed[:, t, :], x_in[ahead.par][:, t, :], ACT.Identity,
                                                     bias=x_stats.nmr[:, t:t + 1], scale=x_stats.rstd[:, t:t + 1])
                        e.then_inc(ly.x_normed, 1)

            for ly in layers:
                over_graphs(act, lambda i, u: iteration(ly, i, u))
                for b in range(2):
                    act.wait_ge(ly.stored[b], DMA * GRAPHS // 2)

        @block.vector
        def _(dve):
            for n, (stage, hi, lo) in enumerate(splits):
                dve.wait_ge(weights_hi, n + 1)
                nc.vector.scalar_tensor_tensor(out=lo[:, :, :], in0=stage, scalar=WSCALE, in1=hi[:, :, :],
                                               op0=ALU.mult, op1=ALU.subtract).then_inc(weights_lo, 1)

            def mean_and_variance(norm, tile, count):
                st = norm.stats
                for t in range(NT):
                    e = nc.vector.bn_stats(st.parts[:, t, :], tile[:, t, :])
                e.then_inc(norm.bn_done, 1)
                dve.wait_ge(norm.bn_done, count)
                dve.sem_inc(dve_passed, 1)
                for t in range(NT):
                    e = nc.vector.bn_aggr(st.mv[:, t, :], st.parts[:, t, :])
                e.then_inc(norm.mv_done, 1)

            def low_part(ly, c):
                g, ps = c.graph, work_ps[c.bank]
                dve.wait_ge(ly.work_hi_done, c.split + 1)
                if c.kind == INPUT_T:
                    e = nc.vector.tensor_tensor(hT_lo[:, :, :], in_two(ps), hT_hi[:, :, :], ALU.subtract)
                elif c.kind == QK:
                    e = nc.vector.scalar_tensor_tensor(out=qk_lo[:, c.index, :], in0=ps[:, :], scalar=1 / WSCALE,
                                                       in1=qk_hi[:, c.index, :], op0=ALU.mult, op1=ALU.subtract)
                elif c.kind == V:
                    flat = v_lo[g.par][:, :, :, :].rearrange("p t h d -> p (t h) d")
                    e = nc.vector.scalar_tensor_tensor(out=flat[:, 8 * c.index:8 * c.index + 8, :], in0=by_head(ps),
                                                       scalar=1 / WSCALE, in1=v_dest(ly, v_hi[g.par], c.index),
                                                       op0=ALU.mult, op1=ALU.subtract)
                else:
                    e = nc.vector.tensor_tensor(attnT_dest(attnT_lo, c.index), in_four(ps),
                                                attnT_dest(attnT_hi, c.index), ALU.subtract)
                e.then_inc(ly.work_read, 1)

            def residual(ly, c):
                g = c.graph
                dve.wait_ge(ly.work_done, c.count + 1)
                dve.wait_ge(ly.res_ready, g.n + 1)
                if due(g.n - 1):
                    dve.wait_ge(ly.finished, g.n - 1)
                nc.vector.scalar_tensor_tensor(out=y[g.par][:, :, :], in0=in_two(work_ps[c.bank]),
                                               scalar=1 / WSCALE, in1=x_res[g.par][:, :, :],
                                               op0=ALU.mult, op1=ALU.add).then_inc(ly.work_read, 1)
                dve.wait_ge(ly.work_read, c.count + 1)
                if due(g.n):
                    dve.wait_ge(ly.y_norm.nmr_done, g.n)
                mean_and_variance(ly.y_norm, y[g.par], g.n + 1)

            def iteration(ly, i, u):
                g, last, ahead = (Graph(i, u + t) for t in (0, -1, 2))
                for h in range(ly.heads):
                    b = h % 2
                    before = chunks_before(ly.plan, ly.heads, i, u, h)
                    if g.live:
                        if h == 0:
                            dve.wait_ge(ly.mask_ready, g.n + 1)
                        n = g.n * ly.heads + h
                        dve.wait_ge(ly.scores_done, n + 1)
                        dve.sem_inc(dve_passed, 1)
                        for qt in range(NT):
                            sc = score_ps[b][:, qt * NODES:(qt + 1) * NODES]
                            e = nc.vector.tensor_tensor_reduce(sc, sc, mask[g.par][:, qt, :], -SCALE, BIG,
                                                               ALU.add, ALU.min, low_max[:, b, qt:qt + 1])
                        e.then_inc(ly.masked, 1)
                    for c in before:
                        if c.kind == OUT:
                            residual(ly, c)
                        else:
                            low_part(ly, c)
                    gt = g if h >= 1 else last
                    if gt.live:
                        n = g.n * ly.heads + h - 1
                        dve.wait_ge(ly.probT_hi_done, n + 1)
                        nc.vector.tensor_tensor(probT_lo[1 - b][:, :, :], in_two(probT_ps[1 - b]),
                                                probT_hi[1 - b][:, :, :], ALU.subtract).then_inc(ly.probT_lo_done, 1)
                    if h % 2 == 1:
                        gv, pair = (g, (h - 2) // 2) if h >= 2 else (last, ly.pairs - 1)
                        if gv.live:
                            k = gv.n * ly.pairs + pair
                            dve.wait_ge(ly.values_done, 2 * k + 2)
                            if due(gv.n - 1) and pair == 0:
                                dve.wait_ge(ly.work_done, read_count(ly.plan, i, u - 2, ATTN_T, ly.pairs // 2 - 1))
                            done = value_ps[pair % 2][:, 0:2 * NT * VW].rearrange("p (t h d) -> p t h d", t=NT, h=2)
                            nc.vector.reciprocal(inv_sum[:, pair % 2], done[:, :, :, HD]).then_inc(ly.inv_done, 1)
                            dve.wait_ge(ly.inv_done, k + 1)
                            dst = attn[gv.par][:, :, pair * P:(pair + 1) * P].rearrange("p t (h d) -> p t h d", h=2)
                            nc.vector.tensor_tensor(dst, done[:, :, :, 0:HD],
                                                    inv_sum[:, pair % 2].unsqueeze(3).broadcast_to([P, NT, 2, HD]),
                                                    ALU.mult).then_inc(ly.attn_done, 1)
                    if h == 1 and ly.with_norm and ahead.live:
                        dve.wait_ge(ly.x_loaded[ahead.par], DMA * (ahead.turn + 1))
                        if due(ahead.n):
                            dve.wait_ge(ly.x_norm.nmr_done, ahead.n)
                        mean_and_variance(ly.x_norm, x_in[ahead.par], ahead.n + 1)

            for ly in layers:
                over_graphs(dve, lambda i, u: iteration(ly, i, u))
                for b in range(2):
                    dve.wait_ge(ly.stored[b], DMA * GRAPHS // 2)

        @block.tensor
        def _(pe):
            def split_product(dst, terms):
                mms = [(a, b) for lhi, llo, rhi, rlo in terms for a, b in ((lhi, rhi), (lhi, rlo), (llo, rhi))]
                for n, (a, b) in enumerate(mms):
                    m = nc.tensor.matmul(dst, a, b, start=n == 0, stop=n == len(mms) - 1)
                return m

            def input_transposed(ly, c):
                g, ps = c.graph, work_ps[c.bank]
                if ly.with_norm:
                    src = h_in[g.par]
                    pe.wait_ge(ly.h_ready, g.n + 1)
                else:
                    src = x_in[g.par]
                    pe.wait_ge(ly.x_loaded[g.par], DMA * (g.turn + 1))
                for t in range(NT):
                    for e in range(ET):
                        at = e * NODES + t * P
                        m = nc.tensor.transpose(ps[:, at:at + P], src[:, t, e * P:(e + 1) * P], ident[:, :])
                return m

            def queries_keys(ly, c):
                for k in range(2):
                    at = k * ly.inner + c.index * P
                    m = split_product(work_ps[c.bank][:, k * NODES:(k + 1) * NODES],
                                      [(ly.w_hi[:, e, at:at + P], ly.w_lo[:, e, at:at + P],
                                        hT_hi[:, e, :], hT_lo[:, e, :]) for e in range(ET)])
                return m

            def values_projected(ly, c):
                tiles = [c.index] if ly.inner == 512 else range(NT)
                for k, t in enumerate(tiles):
                    m = split_product(work_ps[c.bank][:, k * ly.inner:(k + 1) * ly.inner],
                                      [(hT_hi[:, e, t * P:(t + 1) * P], hT_lo[:, e, t * P:(t + 1) * P],
                                        ly.w_hi[:, e, 2 * ly.inner:], ly.w_lo[:, e, 2 * ly.inner:])
                                       for e in range(ET)])
                return m

            def attention_transposed(ly, c):
                if c.index == 0:
                    pe.wait_ge(ly.attn_done, (c.graph.n + 1) * ly.pairs)
                for k in range(4):
                    t, pair = divmod(4 * c.index + k, ly.pairs)
                    m = nc.tensor.transpose(work_ps[c.bank][:, k * P:(k + 1) * P],
                                            attn[c.graph.par][:, t, pair * P:(pair + 1) * P], ident[:, :])
                return m

            def output_product(ly, c):
                for t in range(NT):
                    m = split_product(work_ps[c.bank][:, t * EMB:(t + 1) * EMB],
                                      [(attnT_block(ly, attnT_hi, t, p), attnT_block(ly, attnT_lo, t, p),
                                        ly.wo_hi[:, p, :], ly.wo_lo[:, p, :]) for p in range(ly.pairs)])
                return m

            def work(ly, c, i, u):
                if due(c.count - 1):
                    pe.wait_ge(ly.work_read, c.count - 1)
                if c.kind == INPUT_T:
                    m = input_transposed(ly, c)
                elif c.kind == QK:
                    if c.index == 0:
                        pe.wait_ge(ly.work_read, read_count(ly.plan, i, u + 1, INPUT_T))
                    m = queries_keys(ly, c)
                elif c.kind == V:
                    m = values_projected(ly, c)
                elif c.kind == ATTN_T:
                    m = attention_transposed(ly, c)
                else:
                    pe.wait_ge(ly.work_read, read_count(ly.plan, i, u - 1, ATTN_T, ly.pairs // 2 - 1))
                    m = output_product(ly, c)
                m.then_inc(ly.work_done, 1)

            def scores(ly, g, h):
                n = g.n * ly.heads + h
                if h == 0:
                    pe.wait_ge(ly.stacked, 8 * DMA * (g.n + 1))
                if due(n - 1):
                    pe.wait_ge(ly.probs, n - 1)
                for qt in range(NT):
                    dst = score_ps[h % 2][:, qt * NODES:(qt + 1) * NODES]
                    stack, swap = qk_stack[g.par][:, h % 2, h // 2, :], k_swap[g.par][:, h % 2, h // 2, :]
                    q = stack[:, qt * P:(qt + 1) * P]
                    nc.tensor.matmul(dst, q, stack[:, NODES:], start=True, stop=False)
                    m = nc.tensor.matmul(dst, q, swap, start=False, stop=True)
                m.then_inc(ly.scores_done, 1)

            def transpose_probs(ly, g, h):
                n, b = g.n * ly.heads + h, h % 2
                pe.wait_ge(ly.probs, n + 1)
                if due(n - 1):
                    pe.wait_ge(ly.probT_lo_done, n - 1)
                for qt in range(NT):
                    for kt in range(NT):
                        at = kt * NODES + qt * P
                        m = nc.tensor.transpose(probT_ps[b][:, at:at + P], prob[b][:, qt, kt * P:(kt + 1) * P],
                                                ident[:, :])
                m.then_inc(ly.probT_done, 1)

            def values(ly, g, h):
                n, b, pair = g.n * ly.heads + h, h % 2, h // 2
                pe.wait_ge(ly.probT_lo_done, n + 1)
                if h % 2 == 0:
                    k = g.n * ly.pairs + pair
                    if due(k - 1):
                        pe.wait_ge(ly.attn_done, k - 1)
                for qt in range(NT):
                    at = (qt * 2 + h % 2) * VW
                    dst = value_ps[pair % 2][:, at:at + VW]
                    for kt in range(NT):
                        p_hi = probT_hi[b][:, kt, qt * P:(qt + 1) * P]
                        p_lo = probT_lo[b][:, kt, qt * P:(qt + 1) * P]
                        nc.tensor.matmul(dst, p_hi, v_head(ly, v_hi[g.par], kt, h, VW), start=kt == 0, stop=False)
                        nc.tensor.matmul(dst[:, 0:HD], p_hi, v_head(ly, v_lo[g.par], kt, h, HD),
                                         start=False, stop=False)
                        m = nc.tensor.matmul(dst, p_lo, v_head(ly, v_hi[g.par], kt, h, VW),
                                             start=False, stop=kt == NT - 1)
                m.then_inc(ly.values_done, 1)

            def iteration(ly, i, u):
                g, last = Graph(i, u), Graph(i, u - 1)
                for h in range(ly.heads):
                    if g.live:
                        scores(ly, g, h)
                    gt, ht = (g, h - 1) if h >= 1 else (last, ly.heads - 1)
                    if gt.live:
                        transpose_probs(ly, gt, ht)
                    gv, hv = (g, h - 2) if h >= 2 else (last, ly.heads - 2 + h)
                    if gv.live:
                        values(ly, gv, hv)
                    for c in chunks(ly.plan, i, u, h):
                        work(ly, c, i, u)

            pe.wait_ge(constants, 6)
            pe.wait_ge(weights_lo, len(splits))
            for ly in layers:
                over_graphs(pe, lambda i, u: iteration(ly, i, u))
                for b in range(2):
                    pe.wait_ge(ly.stored[b], DMA * GRAPHS // 2)


def kernel(x, adj, L0_gnn_gamma, L0_gnn_beta, L0_gnn_w_qkv, L0_gnn_w_out, L0_gnn_b_out,
           L1_gnn_Wq, L1_gnn_Wk, L1_gnn_Wv, L1_gnn_Wo, L1_gnn_bo):
    import numpy as np
    import concourse.bacc as bacc
    from concourse.bass_utils import run_bass_kernel_spmd

    given = [("x", x), ("adj", adj), ("gamma", L0_gnn_gamma), ("beta", L0_gnn_beta),
             ("wqkv0", np.asarray(L0_gnn_w_qkv).T), ("wo0", np.asarray(L0_gnn_w_out).T), ("bo0", L0_gnn_b_out),
             ("wq1", L1_gnn_Wq), ("wk1", L1_gnn_Wk), ("wv1", L1_gnn_Wv), ("wo1", L1_gnn_Wo), ("bo1", L1_gnn_bo)]
    nc = bacc.Bacc("TRN2", target_bir_lowering=False, num_devices=1)
    arrays, args = {}, []
    for name, a in given:
        a = np.ascontiguousarray(a)
        arrays[f"in_{name}"] = a
        args.append(nc.dram_tensor(f"in_{name}", a.shape, mybir.dt.from_np(a.dtype), kind="ExternalInput").ap())
    out = nc.dram_tensor("out", (GRAPHS, NODES, EMB), F32, kind="ExternalOutput").ap()
    build(nc, *args, out)
    got = run_bass_kernel_spmd(nc, [arrays], core_ids=[0])
    return got.results[0]["out"]
```

```python
from contextlib import ExitStack

import concourse.bass as bass
from concourse import mybir

F32 = mybir.dt.float32
F16 = mybir.dt.float16
U8 = mybir.dt.uint8
ALU = mybir.AluOpType
ACT = mybir.ActivationFunctionType

P = 128
GRAPHS, NODES, EMB = 32, 256, 256
HD = 64
NT = NODES // P
ET = EMB // P
VW = HD + 1
SCALE = HD ** -0.5
BIG = 3.0e38
WSCALE = 64.0
EPS = 1e-5
DMA = 16


class Graph:

    def __init__(self, i, t):
        self.n = 2 * i + t
        self.turn = i + t // 2
        self.par = t % 2
        self.live = not isinstance(self.n, int) or 0 <= self.n < GRAPHS


INPUT_T, QK, V, ATTN_T, OUT = "input_t", "qk", "v", "attn_t", "out"


class Chunk:

    def __init__(self, plan, i, u, slot):
        _, self.kind, self.index, shift = plan[slot]
        self.t = u + shift
        self.graph = Graph(i, self.t)
        j = 2 * i + u
        if isinstance(j, int):
            before = [kind for jj in range(-3, j + 1) for n, (_, kind, _, shift) in enumerate(plan)
                      if (jj < j or n < slot) and 0 <= jj + shift < GRAPHS]
            self.count, self.split = len(before), len(before) - before.count(OUT)
        else:
            first = Chunk(plan, 2, 0, slot)
            self.count = len(plan) * (j - 4) + first.count
            self.split = (len(plan) - 1) * (j - 4) + first.split
            assert len(plan) % 2 == 0
        self.bank = (self.count if isinstance(self.count, int) else first.count) % 2


def chunks(plan, i, u, step):
    found = [Chunk(plan, i, u, slot) for slot in range(len(plan)) if plan[slot][0] == step]
    return [c for c in found if c.graph.live]


def chunks_before(plan, heads, i, u, step):
    if step:
        return chunks(plan, i, u, step - 1)
    return chunks(plan, i, u - 1, heads - 1) if u else chunks(plan, i - 1, 1, heads - 1)


def read_count(plan, i, t, kind, index=0):
    slot = [(k, x) for _, k, x, _ in plan].index((kind, index))
    t -= plan[slot][3]
    return Chunk(plan, i + t // 2, t % 2, slot).count + 1


def due(count):
    return not isinstance(count, int) or count > 0


def over_graphs(eng, iteration):
    for j in range(-4, 4):
        iteration(j // 2, j % 2)
    with eng.Fori(2, GRAPHS // 2 - 2) as i:
        iteration(i, 0)
        iteration(i, 1)
    for j in range(GRAPHS - 4, GRAPHS + 2):
        iteration(j // 2, j % 2)


def build(nc, x, adj, gamma, beta, wqkv0, wo0, bo0, wq1, wk1, wv1, wo1, bo1, out):
    with ExitStack() as ctx:
        def sb(name, shape, dtype=F32):
            return ctx.enter_context(nc.sbuf_tensor(name, shape, dtype))

        def psum(name):
            return ctx.enter_context(nc.psum_tensor(name, [P, 512], F32))

        def sem(name):
            return ctx.enter_context(nc.semaphore(name))

        score_ps = [psum(f"score_ps{b}") for b in range(2)]
        probT_ps = [psum(f"probT_ps{b}") for b in range(2)]
        value_ps = [psum(f"value_ps{b}") for b in range(2)]
        work_ps = [psum(f"work_ps{b}") for b in range(2)]

        ident = sb("ident", [P, P])
        eps_t = sb("eps_t", [P, NT])
        minus_half = sb("minus_half", [P, NT])
        minus_one = sb("minus_one", [P, NT])
        gamma_b = sb("gamma_b", [P, EMB])
        beta_b = sb("beta_b", [P, EMB])
        mid = sb("mid", [P, GRAPHS, NT, EMB])
        x_in = [sb(f"x_in{b}", [P, NT, EMB]) for b in range(2)]
        x_res = [sb(f"x_res{b}", [P, NT, EMB]) for b in range(2)]
        adj_in = [sb(f"adj_in{b}", [P, NT, NODES], U8) for b in range(2)]
        mask = [sb(f"mask{b}", [P, NT, NODES]) for b in range(2)]
        normed = sb("normed", [P, NT, EMB])
        scaled = sb("scaled", [P, NT, EMB])
        h_in = [sb(f"h_in{b}", [P, NT, EMB]) for b in range(2)]
        hT_hi = [sb(f"hT_hi{b}", [P, ET, NODES], F16) for b in range(2)]
        hT_lo = [sb(f"hT_lo{b}", [P, ET, NODES], F16) for b in range(2)]
        qk_hi = sb("qk_hi", [P, 4, 2 * NODES], F16)
        qk_lo = sb("qk_lo", [P, 4, 2 * NODES], F16)
        qk_stack = [sb(f"qk_stack{b}", [P, 2, 4, 2 * NODES], F16) for b in range(2)]
        k_swap = [sb(f"k_swap{b}", [P, 2, 4, NODES], F16) for b in range(2)]
        v_hi = [sb(f"v_hi{b}", [P, NT, 8, VW], F16) for b in range(2)]
        v_lo = [sb(f"v_lo{b}", [P, NT, 8, HD], F16) for b in range(2)]
        low_max = sb("low_max", [P, 2, NT])
        prob = [sb(f"prob{b}", [P, NT, NODES]) for b in range(2)]
        probT_hi = [sb(f"probT_hi{b}", [P, NT, NODES], F16) for b in range(2)]
        probT_lo = [sb(f"probT_lo{b}", [P, NT, NODES], F16) for b in range(2)]
        inv_sum = sb("inv_sum", [P, 2, NT, 2])
        attn = [sb(f"attn{b}", [P, NT, 8 * HD]) for b in range(2)]
        attnT_hi = sb("attnT_hi", [P, NT, 4, P], F16)
        attnT_lo = sb("attnT_lo", [P, NT, 4, P], F16)
        y = [sb(f"y{b}", [P, NT, EMB]) for b in range(2)]
        y_out = [sb(f"y_out{b}", [P, NT, EMB]) for b in range(2)]

        class Stats:

            def __init__(self, name):
                self.parts = sb(f"{name}_parts", [P, NT, 6])
                self.mv = sb(f"{name}_mv", [P, NT, 2])
                self.vpe = sb(f"{name}_vpe", [P, NT])
                self.rstd = sb(f"{name}_rstd", [P, NT])
                self.mr = sb(f"{name}_mr", [P, NT])
                self.nmr = sb(f"{name}_nmr", [P, NT])

        class Norm:

            def __init__(self, name, stats):
                self.stats = stats
                self.bn_done = sem(f"{name}_bn_done")
                self.mv_done = sem(f"{name}_mv_done")
                self.vpe_done = sem(f"{name}_vpe_done")
                self.rstd_done = sem(f"{name}_rstd_done")
                self.mr_done = sem(f"{name}_mr_done")
                self.nmr_done = sem(f"{name}_nmr_done")

        class Layer:
            def __init__(self, name, heads, with_norm, eye, lookahead, plan):
                self.heads, self.pairs, self.inner = heads, heads // 2, heads * HD
                self.with_norm, self.eye, self.lookahead, self.plan = with_norm, eye, lookahead, plan
                self.qk_shift = next(shift for _, kind, _, shift in plan if kind == QK)
                self.w_hi = sb(f"{name}_w_hi", [P, ET, 3 * self.inner], F16)
                self.w_lo = sb(f"{name}_w_lo", [P, ET, 3 * self.inner], F16)
                self.wo_hi = sb(f"{name}_wo_hi", [P, self.pairs, EMB], F16)
                self.wo_lo = sb(f"{name}_wo_lo", [P, self.pairs, EMB], F16)
                self.bias = sb(f"{name}_bias", [P, EMB])
                self.x_loaded = [sem(f"{name}_x_loaded{b}") for b in range(2)]
                self.adj_loaded = [sem(f"{name}_adj_loaded{b}") for b in range(2)]
                self.res_loaded = [sem(f"{name}_res_loaded{b}") for b in range(2)]
                self.stored = [sem(f"{name}_stored{b}") for b in range(2)]
                self.stacked = sem(f"{name}_stacked")
                self.x_norm = Norm(f"{name}_x", x_stats)
                self.x_normed = sem(f"{name}_x_normed")
                self.x_scaled = sem(f"{name}_x_scaled")
                self.h_ready = sem(f"{name}_h_ready")
                self.res_ready = sem(f"{name}_res_ready")
                self.mask_raw = sem(f"{name}_mask_raw")
                self.mask_ready = sem(f"{name}_mask_ready") if eye else self.mask_raw
                self.y_norm = Norm(f"{name}_y", y_stats)
                self.finished = sem(f"{name}_finished")
                self.work_done = sem(f"{name}_work_done")
                self.work_hi_done = sem(f"{name}_work_hi_done")
                self.work_read = sem(f"{name}_work_read")
                self.scores_done = sem(f"{name}_scores_done")
                self.masked = sem(f"{name}_masked")
                self.probs = sem(f"{name}_probs")
                self.probT_done = sem(f"{name}_probT_done")
                self.probT_hi_done = sem(f"{name}_probT_hi_done")
                self.probT_lo_done = sem(f"{name}_probT_lo_done")
                self.values_done = sem(f"{name}_values_done")
                self.inv_done = sem(f"{name}_inv_done")
                self.attn_done = sem(f"{name}_attn_done")

        x_stats, y_stats = Stats("x_stats"), Stats("y_stats")
        layer0 = Layer("l0", 8, True, True, 3,
                       [(0, QK, 0, 1), (1, QK, 1, 1), (2, QK, 2, 1), (3, QK, 3, 1), (3, ATTN_T, 0, -1),
                        (4, V, 0, 1), (4, ATTN_T, 1, -1), (5, INPUT_T, 0, 2), (6, OUT, 0, -1), (7, V, 1, 1)])
        layer1 = Layer("l1", 4, False, False, 4,
                       [(0, QK, 0, 2), (1, QK, 1, 2), (2, V, 0, 1), (2, ATTN_T, 0, -1),
                        (3, OUT, 0, -1), (3, INPUT_T, 0, 3)])
        layers = (layer0, layer1)

        stage0 = mid[:, 20:26].rearrange("p g t e -> p (g t e)").rearrange("p (c n) -> p c n", c=ET)
        stage_o0 = mid[:, 26:28].rearrange("p g t e -> p (g t) e")
        stage1 = mid[:, 28:31].rearrange("p g t e -> p (g t e)").rearrange("p (c n) -> p c n", c=ET)
        stage_o1 = mid[:, 31:32].rearrange("p g t e -> p (g t) e")
        weights_loaded = [sem(f"weights_loaded{n}") for n in range(4)]
        biases_loaded = sem("biases_loaded")
        weights_hi = sem("weights_hi")
        weights_lo = sem("weights_lo")
        zeroed = sem("zeroed")
        constants = sem("constants")
        sp_passed, pool_passed, dve_passed = sem("sp_passed"), sem("pool_passed"), sem("dve_passed")
        splits = [(stage0, layer0.w_hi, layer0.w_lo), (stage_o0, layer0.wo_hi, layer0.wo_lo),
                  (stage1, layer1.w_hi, layer1.w_lo), (stage_o1, layer1.wo_hi, layer1.wo_lo)]
        WEIGHT_DMAS = (1, 1, 3, 1)

        def nodes_of(array, g):
            return array[bass.ds(g.n, 1)].rearrange("g (t p) c -> p (g t) c", p=P)

        def mid_of(g):
            return mid[:, bass.ds(g.n, 1)].rearrange("p g t e -> p (g t) e")

        def in_two(ps):
            return ps[:, :].rearrange("p (c n) -> p c n", c=2)

        def in_four(ps):
            return ps[:, :].rearrange("p (r n) -> p r n", n=P)

        def by_head(ps):
            return ps[:, :].rearrange("p (h d) -> p h d", d=HD)

        def v_dest(ly, tile, c):
            flat = tile[:, :, :, :].rearrange("p t h d -> p (t h) d")
            return flat[:, 8 * c:8 * c + 8, 0:HD]

        def v_head(ly, tile, kt, head, width):
            flat = tile[:, :, :, :].rearrange("p t h d -> p (t h) d")
            return flat[:, kt * ly.heads + head, 0:width]

        def attnT_dest(tile, c):
            flat = tile[:, :, :, :].rearrange("p t r n -> p (t r) n")
            return flat[:, 4 * c:4 * c + 4, :]

        def attnT_block(ly, tile, t, pair):
            flat = tile[:, :, :, :].rearrange("p t r n -> p (t r) n")
            return flat[:, t * ly.pairs + pair, :]

        FINISH_STEP, INPUT_NORM_STEP = 2, 3

        block = ctx.enter_context(nc.Block())

        @block.sync
        def _(sp):
            by_row = "(c p) n -> p c n"
            sp.dma_start(stage0, wqkv0.rearrange(by_row, p=P)).then_inc(weights_loaded[0], DMA)

            for tile, row in ((gamma_b, gamma), (beta_b, beta), (layer0.bias, bo0), (layer1.bias, bo1)):
                sp.dma_start(tile[:, :], row.partition_broadcast(P)).then_inc(biases_loaded, DMA)
            sp.dma_start(stage_o0, wo0.rearrange(by_row, p=P)).then_inc(weights_loaded[1], DMA)
            for n, w in enumerate((wq1, wk1, wv1)):
                sp.dma_start(stage1[:, :, n * layer1.inner:(n + 1) * layer1.inner],
                             w.rearrange(by_row, p=P)).then_inc(weights_loaded[2], DMA)
            sp.dma_start(stage_o1, wo1.rearrange(by_row, p=P)).then_inc(weights_loaded[3], DMA)

            def iteration(ly, i, u):
                g = Graph(i, u + ly.lookahead)
                if g.live:
                    if due(g.n - 1):
                        if ly.with_norm:
                            sp.wait_ge(ly.x_normed, g.n - 1)
                        else:
                            sp.wait_ge(ly.work_done, read_count(ly.plan, i, u + ly.lookahead - 2, INPUT_T))
                    src = nodes_of(x, g) if ly is layer0 else mid_of(g)
                    sp.dma_start(x_in[g.par][:, :, :], src).then_inc(ly.x_loaded[g.par], DMA)
                g = Graph(i, u + 2)
                if g.live:
                    if due(g.n - 1):
                        sp.wait_ge(ly.mask_raw, g.n - 1)
                        sp.sem_inc(sp_passed, 1)
                    sp.dma_start(adj_in[g.par][:, :, :], nodes_of(adj, g)).then_inc(ly.adj_loaded[g.par], DMA)
                g = Graph(i, u)
                if g.live:
                    if due(g.n - 1):
                        sp.wait_ge(ly.work_read, read_count(ly.plan, i, u - 2, OUT))
                    src = nodes_of(x, g) if ly is layer0 else mid_of(g)
                    sp.dma_start(x_res[g.par][:, :, :], src).then_inc(ly.res_loaded[g.par], DMA)
                t = u + ly.qk_shift
                g = Graph(i, t)
                if g.live:
                    sp.wait_ge(ly.work_read, read_count(ly.plan, i, t, QK, ly.pairs - 1))
                    sp.sem_inc(sp_passed, 1)
                    if due((g.n - 1) * ly.heads):
                        sp.wait_ge(ly.scores_done, (g.n - 1) * ly.heads)
                        sp.sem_inc(sp_passed, 1)
                    for half in range(2):
                        rows, all_pairs = slice(HD * half, HD * half + HD), slice(0, ly.pairs)
                        stack, swap = qk_stack[g.par][:, half, all_pairs, :], k_swap[g.par][:, half, all_pairs, :]
                        for dst, src in ((stack[0:HD], qk_hi[rows, all_pairs, :]),
                                         (stack[HD:P], qk_lo[rows, all_pairs, :]),
                                         (swap[0:HD], qk_lo[rows, all_pairs, NODES:2 * NODES]),
                                         (swap[HD:P], qk_hi[rows, all_pairs, NODES:2 * NODES])):
                            sp.dma_start(dst, src).then_inc(ly.stacked, DMA)
                g = Graph(i, u - 2)
                if g.live:
                    if ly is layer0 and isinstance(g.n, int) and g.n == 0:
                        sp.wait_ge(weights_lo, len(splits))
                    sp.wait_ge(ly.finished, g.n + 1)
                    dst = mid_of(g) if ly is layer0 else nodes_of(out, g)
                    sp.dma_start(dst, y_out[g.par][:, :, :]).then_inc(ly.stored[g.par], DMA)

            for ly in layers:
                over_graphs(sp, lambda i, u: iteration(ly, i, u))
                for b in range(2):
                    sp.wait_ge(ly.stored[b], DMA * GRAPHS // 2)

        @block.gpsimd
        def _(pool):
            nc.gpsimd.memset(ident[:, :], 0.0).then_inc(zeroed, 1)
            pool.wait_ge(zeroed, 1)
            nc.gpsimd.affine_select(out=ident[:, :], in_=ident[:, :], compare_op=ALU.not_equal, fill=1.0, base=0,
                                    pattern=[[-1, P]], channel_multiplier=1).then_inc(constants, 1)
            nc.gpsimd.memset(eps_t[:, :], EPS).then_inc(constants, 1)
            nc.gpsimd.memset(minus_half[:, :], -0.5).then_inc(constants, 1)
            nc.gpsimd.memset(minus_one[:, :], -1.0).then_inc(constants, 1)
            for b in range(2):
                nc.gpsimd.memset(v_hi[b][:, :, :, HD:VW], 1.0).then_inc(constants, 1)
            pool.wait_ge(constants, 6)
            pool.wait_ge(biases_loaded, 4 * DMA)

            def normaliser(norm, count):
                st = norm.stats
                nc.gpsimd.tensor_tensor(st.vpe[:, :], st.mv[:, :, 1], eps_t[:, :], ALU.add).then_inc(norm.vpe_done, 1)
                pool.wait_ge(norm.vpe_done, count)
                nc.gpsimd.tensor_tensor(st.rstd[:, :], st.vpe[:, :], minus_half[:, :],
                                        ALU.pow).then_inc(norm.rstd_done, 1)
                pool.wait_ge(norm.rstd_done, count)
                nc.gpsimd.tensor_tensor(st.mr[:, :], st.mv[:, :, 0], st.rstd[:, :],
                                        ALU.mult).then_inc(norm.mr_done, 1)
                pool.wait_ge(norm.mr_done, count)
                nc.gpsimd.tensor_tensor(st.nmr[:, :], st.mr[:, :], minus_one[:, :],
                                        ALU.mult).then_inc(norm.nmr_done, 1)

            def wide(row):
                return row[:, :].unsqueeze(1).broadcast_to([P, NT, EMB])

            def iteration(ly, i, u):
                g = Graph(i, u + 1)
                if g.live:
                    pool.wait_ge(ly.adj_loaded[g.par], DMA * (g.turn + 1))
                    if due((g.n - 1) * ly.heads):
                        pool.wait_ge(ly.masked, (g.n - 1) * ly.heads)
                    pool.sem_inc(pool_passed, 1)
                    nc.gpsimd.tensor_scalar(mask[g.par][:, :, :], adj_in[g.par][:, :, :], BIG, BIG,
                                            ALU.mult, ALU.subtract).then_inc(ly.mask_raw, 1)
                    if ly.eye:
                        pool.wait_ge(ly.mask_raw, g.n + 1)
                        pool.sem_inc(pool_passed, 1)
                        nc.gpsimd.affine_select(out=mask[g.par][:, :, :], in_=mask[g.par][:, :, :],
                                                compare_op=ALU.not_equal, fill=0.0, base=0,
                                                pattern=[[P, NT], [-1, NODES]],
                                                channel_multiplier=1).then_inc(ly.mask_ready, 1)
                g = Graph(i, u - 2)
                if g.live:
                    pool.wait_ge(ly.y_norm.mv_done, g.n + 1)
                    if due(g.n):
                        pool.wait_ge(ly.finished, g.n)
                    normaliser(ly.y_norm, g.n + 1)
                g = Graph(i, u)
                if g.live:
                    pool.wait_ge(ly.res_loaded[g.par], DMA * (g.turn + 1))
                    nc.gpsimd.tensor_tensor(x_res[g.par][:, :, :], x_res[g.par][:, :, :], wide(ly.bias),
                                            ALU.add).then_inc(ly.res_ready, 1)
                g = Graph(i, u + 2)
                if ly.with_norm and g.live:
                    pool.wait_ge(ly.x_norm.mv_done, g.n + 1)
                    if due(g.n):
                        pool.wait_ge(ly.x_normed, g.n)
                    normaliser(ly.x_norm, g.n + 1)
                    pool.wait_ge(ly.x_normed, g.n + 1)
                    nc.gpsimd.tensor_tensor(scaled[:, :, :], normed[:, :, :], wide(gamma_b),
                                            ALU.mult).then_inc(ly.x_scaled, 1)
                    pool.wait_ge(ly.x_scaled, g.n + 1)
                    if due(g.n - 1):
                        pool.wait_ge(ly.work_done, read_count(ly.plan, i, u, INPUT_T))
                    nc.gpsimd.tensor_tensor(h_in[g.par][:, :, :], scaled[:, :, :], wide(beta_b),
                                            ALU.add).then_inc(ly.h_ready, 1)

            for ly in layers:
                over_graphs(pool, lambda i, u: iteration(ly, i, u))
                for b in range(2):
                    pool.wait_ge(ly.stored[b], DMA * GRAPHS // 2)

        @block.scalar
        def _(act):
            for n, (stage, hi, _) in enumerate(splits):
                act.wait_ge(weights_loaded[n], WEIGHT_DMAS[n] * DMA)
                nc.scalar.activation(hi[:, :, :], stage, ACT.Copy, scale=WSCALE).then_inc(weights_hi, 1)

            def high_part(ly, c):
                g, ps = c.graph, work_ps[c.bank]
                act.wait_ge(ly.work_done, c.count + 1)
                if c.kind == INPUT_T:
                    e = nc.scalar.activation(hT_hi[g.par][:, :, :], in_two(ps), ACT.Copy)
                elif c.kind == QK:
                    if c.index == 0 and due(g.n):
                        act.wait_ge(ly.stacked, 8 * DMA * g.n)
                    e = nc.scalar.activation(qk_hi[:, c.index, :], ps[:, :], ACT.Copy, scale=1 / WSCALE)
                elif c.kind == V:
                    if due((g.n - 1) * ly.heads):
                        act.wait_ge(ly.values_done, (g.n - 1) * ly.heads)
                    e = nc.scalar.activation(v_dest(ly, v_hi[g.par], c.index), by_head(ps), ACT.Copy,
                                             scale=1 / WSCALE)
                else:
                    e = nc.scalar.activation(attnT_dest(attnT_hi, c.index), in_four(ps), ACT.Copy)
                e.then_inc(ly.work_hi_done, 1)

            def iteration(ly, i, u):
                g, last, older, ahead = (Graph(i, u + t) for t in (0, -1, -2, 2))
                for h in range(ly.heads):
                    b = h % 2
                    for c in chunks_before(ly.plan, ly.heads, i, u, h):
                        if c.kind != OUT:
                            high_part(ly, c)
                    gt = g if h >= 1 else last
                    if gt.live:
                        n = g.n * ly.heads + h - 1
                        act.wait_ge(ly.probT_done, n + 1)
                        if due(n - 1):
                            act.wait_ge(ly.values_done, n - 1)
                        nc.scalar.activation(probT_hi[1 - b][:, :, :], in_two(probT_ps[1 - b]),
                                             ACT.Copy).then_inc(ly.probT_hi_done, 1)
                    if g.live:
                        n = g.n * ly.heads + h
                        act.wait_ge(ly.masked, n + 1)
                        if due(n - 1):
                            act.wait_ge(ly.probT_done, n - 1)
                        for qt in range(NT):
                            e = nc.scalar.activation(prob[b][:, qt, :],
                                                     score_ps[b][:, qt * NODES:(qt + 1) * NODES],
                                                     ACT.Exp, bias=low_max[:, b, qt:qt + 1], scale=-1.0)
                        e.then_inc(ly.probs, 1)
                    if h == FINISH_STEP and older.live:
                        act.wait_ge(ly.y_norm.nmr_done, older.n + 1)
                        if due(older.turn):
                            act.wait_ge(ly.stored[older.par], DMA * older.turn)
                        for t in range(NT):
                            e = nc.scalar.activation(y_out[older.par][:, t, :], y[older.par][:, t, :], ACT.Identity,
                                                     bias=y_stats.nmr[:, t:t + 1], scale=y_stats.rstd[:, t:t + 1])
                        e.then_inc(ly.finished, 1)
                    if h == INPUT_NORM_STEP and ly.with_norm and ahead.live:
                        act.wait_ge(ly.x_norm.nmr_done, ahead.n + 1)
                        if due(ahead.n):
                            act.wait_ge(ly.x_scaled, ahead.n)
                        for t in range(NT):
                            e = nc.scalar.activation(normed[:, t, :], x_in[ahead.par][:, t, :], ACT.Identity,
                                                     bias=x_stats.nmr[:, t:t + 1], scale=x_stats.rstd[:, t:t + 1])
                        e.then_inc(ly.x_normed, 1)

            for ly in layers:
                over_graphs(act, lambda i, u: iteration(ly, i, u))
                for b in range(2):
                    act.wait_ge(ly.stored[b], DMA * GRAPHS // 2)

        @block.vector
        def _(dve):
            for n, (stage, hi, lo) in enumerate(splits):
                dve.wait_ge(weights_hi, n + 1)
                nc.vector.scalar_tensor_tensor(out=lo[:, :, :], in0=stage, scalar=WSCALE, in1=hi[:, :, :],
                                               op0=ALU.mult, op1=ALU.subtract).then_inc(weights_lo, 1)

            def partial_statistics(norm, tile):
                for t in range(NT):
                    e = nc.vector.bn_stats(norm.stats.parts[:, t, :], tile[:, t, :])
                e.then_inc(norm.bn_done, 1)

            def mean_and_variance(norm, count):
                st = norm.stats
                if due(count - 1):
                    dve.wait_ge(norm.nmr_done, count - 1)
                dve.wait_ge(norm.bn_done, count)
                dve.sem_inc(dve_passed, 1)
                for t in range(NT):
                    e = nc.vector.bn_aggr(st.mv[:, t, :], st.parts[:, t, :])
                e.then_inc(norm.mv_done, 1)

            def low_part(ly, c):
                g, ps = c.graph, work_ps[c.bank]
                dve.wait_ge(ly.work_hi_done, c.split + 1)
                if c.kind == INPUT_T:
                    e = nc.vector.tensor_tensor(hT_lo[g.par][:, :, :], in_two(ps), hT_hi[g.par][:, :, :], ALU.subtract)
                elif c.kind == QK:
                    e = nc.vector.scalar_tensor_tensor(out=qk_lo[:, c.index, :], in0=ps[:, :], scalar=1 / WSCALE,
                                                       in1=qk_hi[:, c.index, :], op0=ALU.mult, op1=ALU.subtract)
                elif c.kind == V:
                    flat = v_lo[g.par][:, :, :, :].rearrange("p t h d -> p (t h) d")
                    e = nc.vector.scalar_tensor_tensor(out=flat[:, 8 * c.index:8 * c.index + 8, :], in0=by_head(ps),
                                                       scalar=1 / WSCALE, in1=v_dest(ly, v_hi[g.par], c.index),
                                                       op0=ALU.mult, op1=ALU.subtract)
                else:
                    e = nc.vector.tensor_tensor(attnT_dest(attnT_lo, c.index), in_four(ps),
                                                attnT_dest(attnT_hi, c.index), ALU.subtract)
                e.then_inc(ly.work_read, 1)

            def residual(ly, c):
                g = c.graph
                dve.wait_ge(ly.work_done, c.count + 1)
                dve.wait_ge(ly.res_ready, g.n + 1)
                if due(g.n - 1):
                    dve.wait_ge(ly.finished, g.n - 1)
                nc.vector.scalar_tensor_tensor(out=y[g.par][:, :, :], in0=in_two(work_ps[c.bank]),
                                               scalar=1 / WSCALE, in1=x_res[g.par][:, :, :],
                                               op0=ALU.mult, op1=ALU.add).then_inc(ly.work_read, 1)
                dve.wait_ge(ly.work_read, c.count + 1)
                partial_statistics(ly.y_norm, y[g.par])

            def iteration(ly, i, u):
                g, nxt, last, ahead = (Graph(i, u + t) for t in (0, 1, -1, 2))
                for h in range(ly.heads):
                    b = h % 2
                    before = chunks_before(ly.plan, ly.heads, i, u, h)
                    for c in before:
                        if c.kind == OUT:
                            residual(ly, c)
                        else:
                            low_part(ly, c)
                    gt = g if h >= 1 else last
                    if gt.live:
                        n = g.n * ly.heads + h - 1
                        dve.wait_ge(ly.probT_hi_done, n + 1)
                        nc.vector.tensor_tensor(probT_lo[1 - b][:, :, :], in_two(probT_ps[1 - b]),
                                                probT_hi[1 - b][:, :, :], ALU.subtract).then_inc(ly.probT_lo_done, 1)
                    gv, pair = (g, (h - 2) // 2) if h >= 2 else (last, ly.pairs - 1)
                    pair_complete = h % 2 == 1 and gv.live
                    if pair_complete:
                        k = gv.n * ly.pairs + pair
                        done = value_ps[pair % 2][:, 0:2 * NT * VW].rearrange("p (t h d) -> p t h d", t=NT, h=2)
                        dve.wait_ge(ly.values_done, 2 * k + 2)
                        nc.vector.reciprocal(inv_sum[:, pair % 2], done[:, :, :, HD]).then_inc(ly.inv_done, 1)
                    gs, hs = (g, h + 1) if h + 1 < ly.heads else (nxt, 0)
                    if gs.live:
                        if hs == 0:
                            dve.wait_ge(ly.mask_ready, gs.n + 1)
                        dve.wait_ge(ly.scores_done, g.n * ly.heads + h + 2)
                        dve.sem_inc(dve_passed, 1)
                        for qt in range(NT):
                            sc = score_ps[1 - b][:, qt * NODES:(qt + 1) * NODES]
                            e = nc.vector.tensor_tensor_reduce(sc, sc, mask[gs.par][:, qt, :], -SCALE, BIG,
                                                               ALU.add, ALU.min, low_max[:, 1 - b, qt:qt + 1])
                        e.then_inc(ly.masked, 1)
                    if pair_complete:
                        dve.wait_ge(ly.inv_done, k + 1)
                        if due(gv.n - 1) and pair == 0:
                            dve.wait_ge(ly.work_done, read_count(ly.plan, i, u - 2, ATTN_T, ly.pairs // 2 - 1))
                        dst = attn[gv.par][:, :, pair * P:(pair + 1) * P].rearrange("p t (h d) -> p t h d", h=2)
                        nc.vector.tensor_tensor(dst, done[:, :, :, 0:HD],
                                                inv_sum[:, pair % 2].unsqueeze(3).broadcast_to([P, NT, 2, HD]),
                                                ALU.mult).then_inc(ly.attn_done, 1)
                    for c in before:
                        if c.kind == OUT:
                            mean_and_variance(ly.y_norm, c.graph.n + 1)
                    if ly.with_norm and ahead.live:
                        if h == 1:
                            dve.wait_ge(ly.x_loaded[ahead.par], DMA * (ahead.turn + 1))
                            partial_statistics(ly.x_norm, x_in[ahead.par])
                        if h == 2:
                            mean_and_variance(ly.x_norm, ahead.n + 1)

            for ly in layers:
                over_graphs(dve, lambda i, u: iteration(ly, i, u))
                for b in range(2):
                    dve.wait_ge(ly.stored[b], DMA * GRAPHS // 2)

        @block.tensor
        def _(pe):
            def split_product(dst, terms):
                mms = [(a, b) for lhi, llo, rhi, rlo in terms for a, b in ((lhi, rhi), (lhi, rlo), (llo, rhi))]
                for n, (a, b) in enumerate(mms):
                    m = nc.tensor.matmul(dst, a, b, start=n == 0, stop=n == len(mms) - 1)
                return m

            def input_transposed(ly, c):
                g, ps = c.graph, work_ps[c.bank]
                if ly.with_norm:
                    src = h_in[g.par]
                    pe.wait_ge(ly.h_ready, g.n + 1)
                else:
                    src = x_in[g.par]
                    pe.wait_ge(ly.x_loaded[g.par], DMA * (g.turn + 1))
                for t in range(NT):
                    for e in range(ET):
                        at = e * NODES + t * P
                        m = nc.tensor.transpose(ps[:, at:at + P], src[:, t, e * P:(e + 1) * P], ident[:, :])
                return m

            def queries_keys(ly, c):
                for k in range(2):
                    at = k * ly.inner + c.index * P
                    m = split_product(work_ps[c.bank][:, k * NODES:(k + 1) * NODES],
                                      [(ly.w_hi[:, e, at:at + P], ly.w_lo[:, e, at:at + P],
                                        hT_hi[c.graph.par][:, e, :], hT_lo[c.graph.par][:, e, :]) for e in range(ET)])
                return m

            def values_projected(ly, c):
                tiles = [c.index] if ly.inner == 512 else range(NT)
                for k, t in enumerate(tiles):
                    m = split_product(work_ps[c.bank][:, k * ly.inner:(k + 1) * ly.inner],
                                      [(hT_hi[c.graph.par][:, e, t * P:(t + 1) * P], hT_lo[c.graph.par][:, e, t * P:(t + 1) * P],
                                        ly.w_hi[:, e, 2 * ly.inner:], ly.w_lo[:, e, 2 * ly.inner:])
                                       for e in range(ET)])
                return m

            def attention_transposed(ly, c):
                if c.index == 0:
                    pe.wait_ge(ly.attn_done, (c.graph.n + 1) * ly.pairs)
                for k in range(4):
                    t, pair = divmod(4 * c.index + k, ly.pairs)
                    m = nc.tensor.transpose(work_ps[c.bank][:, k * P:(k + 1) * P],
                                            attn[c.graph.par][:, t, pair * P:(pair + 1) * P], ident[:, :])
                return m

            def output_product(ly, c):
                for t in range(NT):
                    m = split_product(work_ps[c.bank][:, t * EMB:(t + 1) * EMB],
                                      [(attnT_block(ly, attnT_hi, t, p), attnT_block(ly, attnT_lo, t, p),
                                        ly.wo_hi[:, p, :], ly.wo_lo[:, p, :]) for p in range(ly.pairs)])
                return m

            def work(ly, c, i):
                if due(c.count - 1):
                    pe.wait_ge(ly.work_read, c.count - 1)
                if c.kind == INPUT_T:
                    m = input_transposed(ly, c)
                elif c.kind == QK:
                    if c.index == 0:
                        pe.wait_ge(ly.work_read, read_count(ly.plan, i, c.t, INPUT_T))
                    m = queries_keys(ly, c)
                elif c.kind == V:
                    m = values_projected(ly, c)
                elif c.kind == ATTN_T:
                    m = attention_transposed(ly, c)
                else:
                    pe.wait_ge(ly.work_read, read_count(ly.plan, i, c.t, ATTN_T, ly.pairs // 2 - 1))
                    m = output_product(ly, c)
                m.then_inc(ly.work_done, 1)

            def scores(ly, g, h):
                n = g.n * ly.heads + h
                if h == 0:
                    pe.wait_ge(ly.stacked, 8 * DMA * (g.n + 1))
                if due(n - 1):
                    pe.wait_ge(ly.probs, n - 1)
                for qt in range(NT):
                    dst = score_ps[h % 2][:, qt * NODES:(qt + 1) * NODES]
                    stack, swap = qk_stack[g.par][:, h % 2, h // 2, :], k_swap[g.par][:, h % 2, h // 2, :]
                    q = stack[:, qt * P:(qt + 1) * P]
                    nc.tensor.matmul(dst, q, stack[:, NODES:], start=True, stop=False)
                    m = nc.tensor.matmul(dst, q, swap, start=False, stop=True)
                m.then_inc(ly.scores_done, 1)

            def transpose_probs(ly, g, h):
                n, b = g.n * ly.heads + h, h % 2
                pe.wait_ge(ly.probs, n + 1)
                if due(n - 1):
                    pe.wait_ge(ly.probT_lo_done, n - 1)
                for qt in range(NT):
                    for kt in range(NT):
                        at = kt * NODES + qt * P
                        m = nc.tensor.transpose(probT_ps[b][:, at:at + P], prob[b][:, qt, kt * P:(kt + 1) * P],
                                                ident[:, :])
                m.then_inc(ly.probT_done, 1)

            def values(ly, g, h):
                n, b, pair = g.n * ly.heads + h, h % 2, h // 2
                pe.wait_ge(ly.probT_lo_done, n + 1)
                if h % 2 == 0:
                    k = g.n * ly.pairs + pair
                    if due(k - 1):
                        pe.wait_ge(ly.attn_done, k - 1)
                for qt in range(NT):
                    at = (qt * 2 + h % 2) * VW
                    dst = value_ps[pair % 2][:, at:at + VW]
                    for kt in range(NT):
                        p_hi = probT_hi[b][:, kt, qt * P:(qt + 1) * P]
                        p_lo = probT_lo[b][:, kt, qt * P:(qt + 1) * P]
                        nc.tensor.matmul(dst, p_hi, v_head(ly, v_hi[g.par], kt, h, VW), start=kt == 0, stop=False)
                        nc.tensor.matmul(dst[:, 0:HD], p_hi, v_head(ly, v_lo[g.par], kt, h, HD),
                                         start=False, stop=False)
                        m = nc.tensor.matmul(dst, p_lo, v_head(ly, v_hi[g.par], kt, h, VW),
                                             start=False, stop=kt == NT - 1)
                m.then_inc(ly.values_done, 1)

            def iteration(ly, i, u):
                g, nxt, last = Graph(i, u), Graph(i, u + 1), Graph(i, u - 1)
                for h in range(ly.heads):
                    gt, ht = (g, h - 1) if h >= 1 else (last, ly.heads - 1)
                    if gt.live:
                        transpose_probs(ly, gt, ht)
                    gs, hs = (g, h + 1) if h + 1 < ly.heads else (nxt, 0)
                    if gs.live:
                        scores(ly, gs, hs)
                    gv, hv = (g, h - 2) if h >= 2 else (last, ly.heads - 2 + h)
                    if gv.live:
                        values(ly, gv, hv)
                    for c in chunks(ly.plan, i, u, h):
                        work(ly, c, i)

            pe.wait_ge(constants, 6)
            for n, ly in enumerate(layers):
                pe.wait_ge(weights_lo, 2 * n + 2)
                over_graphs(pe, lambda i, u: iteration(ly, i, u))
                for b in range(2):
                    pe.wait_ge(ly.stored[b], DMA * GRAPHS // 2)


def kernel(x, adj, L0_gnn_gamma, L0_gnn_beta, L0_gnn_w_qkv, L0_gnn_w_out, L0_gnn_b_out,
           L1_gnn_Wq, L1_gnn_Wk, L1_gnn_Wv, L1_gnn_Wo, L1_gnn_bo):
    import numpy as np
    import concourse.bacc as bacc
    from concourse.bass_utils import run_bass_kernel_spmd

    given = [("x", x), ("adj", adj), ("gamma", L0_gnn_gamma), ("beta", L0_gnn_beta),
             ("wqkv0", np.asarray(L0_gnn_w_qkv).T), ("wo0", np.asarray(L0_gnn_w_out).T), ("bo0", L0_gnn_b_out),
             ("wq1", L1_gnn_Wq), ("wk1", L1_gnn_Wk), ("wv1", L1_gnn_Wv), ("wo1", L1_gnn_Wo), ("bo1", L1_gnn_bo)]
    nc = bacc.Bacc("TRN2", target_bir_lowering=False, num_devices=1)
    arrays, args = {}, []
    for name, a in given:
        a = np.ascontiguousarray(a)
        arrays[f"in_{name}"] = a
        args.append(nc.dram_tensor(f"in_{name}", a.shape, mybir.dt.from_np(a.dtype), kind="ExternalInput").ap())
    out = nc.dram_tensor("out", (GRAPHS, NODES, EMB), F32, kind="ExternalOutput").ap()
    build(nc, *args, out)
    got = run_bass_kernel_spmd(nc, [arrays], core_ids=[0])
    return got.results[0]["out"]
```

```python
from contextlib import ExitStack

import concourse.bass as bass
from concourse import mybir

F32 = mybir.dt.float32
F16 = mybir.dt.float16
U8 = mybir.dt.uint8
ALU = mybir.AluOpType
ACT = mybir.ActivationFunctionType

P = 128
GRAPHS, NODES, EMB = 32, 256, 256
HD = 64
NT = NODES // P
ET = EMB // P
VW = HD + 1
SCALE = HD ** -0.5
BIG = 3.0e38
WSCALE = 64.0
EPS = 1e-5
DMA = 16


INPUT_T, QK, V, ATTN_T, OUT_BEGIN, OUT = "input_t", "qk", "v", "attn_t", "out_begin", "out"
ALL = 2 * GRAPHS
FIRST_J, LAST_J = -3, ALL + 1
PEEL = 4


class Layer:

    def __init__(self, index, heads, heads_before, plan):
        self.index, self.heads, self.pairs, self.inner, self.plan = index, heads, heads // 2, heads * HD, plan
        self.first = index * GRAPHS
        self.head_base = heads_before - self.first * heads


LAYER0 = Layer(0, 8, 0,
               [(0, QK, 0, 1), (1, QK, 1, 1), (2, QK, 2, 1), (3, QK, 3, 1), (3, ATTN_T, 0, -1),
                (4, V, 0, 1), (4, ATTN_T, 1, -1), (5, INPUT_T, 0, 2), (5, OUT_BEGIN, 0, -1),
                (6, OUT, 0, -1), (7, V, 1, 1)])
LAYER1 = Layer(1, 4, 8 * GRAPHS,
               [(0, QK, 0, 2), (1, V, 0, 1), (1, INPUT_T, 0, 3), (2, ATTN_T, 0, -1), (2, QK, 1, 2),
                (3, OUT, 0, -1)])
LAYERS = (LAYER0, LAYER1)
TRANSITION = {GRAPHS - 1: [(0, QK, 0, 1), (1, QK, 1, 1), (2, INPUT_T, 0, 2), (3, ATTN_T, 0, -1),
                           (3, ATTN_T, 1, -1), (4, V, 0, 1), (5, OUT, 0, -1), (6, QK, 0, 2), (7, QK, 1, 2),
                           (7, INPUT_T, 0, 3)],
              GRAPHS: [(0, QK, 0, 2), (1, V, 0, 1), (1, INPUT_T, 0, 3), (2, ATTN_T, 0, -1), (2, ATTN_T, 1, -1),
                       (2, QK, 1, 2), (3, OUT, 0, -1)]}


class Iteration:

    def __init__(self, i, u, layer=None):
        self.i, self.u, self.j = i, u, 2 * i + u
        self.fixed = isinstance(self.j, int)
        self.layer = layer or LAYERS[self.j >= GRAPHS]

    def plan(self):
        return TRANSITION.get(self.j, self.layer.plan) if self.fixed else self.layer.plan

    def before(self):
        return iteration_of(self.j - 1) if self.fixed else Iteration(self.i, self.u - 1, self.layer)


def iteration_of(j):
    return Iteration(j // 2, j % 2)


class Graph:

    def __init__(self, it, t):
        self.it, self.t = it, t
        t += it.u
        self.n, self.turn, self.par = 2 * it.i + t, it.i + t // 2, t % 2
        self.live = not it.fixed or 0 <= self.n < ALL
        self.layer = LAYERS[self.n >= GRAPHS] if it.fixed else it.layer
        self.index = self.n - self.layer.first

    def head(self, h):
        return self.n * self.layer.heads + self.layer.head_base + h

    def pair(self, p):
        return self.n * self.layer.pairs + self.layer.head_base // 2 + p

    def after(self, t):
        return Graph(self.it, self.t + t)

    def is_number(self, n):
        return self.it.fixed and self.n == n


def chunk_order():
    order = [(kind, index, it.j + shift) for it in map(iteration_of, range(FIRST_J, LAST_J + 1))
             for _, kind, index, shift in it.plan() if kind != OUT_BEGIN and 0 <= it.j + shift < ALL]
    split = [key for key in order if key[0] != OUT]
    return {key: n for n, key in enumerate(order)}, {key: n for n, key in enumerate(split)}


PLACE, SPLIT_PLACE = chunk_order()


def place(kind, index, graph, places=PLACE):
    if graph.it.fixed:
        return places.get((kind, index, graph.n), -1)
    ly, steady = graph.layer, graph.layer.first + 8
    each = places[kind, index, steady + 1] - places[kind, index, steady]
    return each * (graph.n - steady) + places[kind, index, steady]


def through(kind, index, graph):
    return place(kind, index, graph) + 1


class Chunk:

    def __init__(self, it, step, kind, index, shift):
        self.step, self.kind, self.index, self.graph = step, kind, index, Graph(it, shift)
        self.count = place(kind, index, self.graph)
        self.split = place(kind, index, self.graph, SPLIT_PLACE) if kind != OUT else None
        known = self.graph.n if it.fixed else it.layer.first + 8
        self.bank = PLACE.get((kind, index, known), 0) % 2


def chunks(it, step):
    found = [Chunk(it, *entry) for entry in it.plan() if entry[0] == step and entry[1] != OUT_BEGIN]
    return [c for c in found if c.graph.live]


def chunks_and_begins(it, step):
    found = [(Chunk(it, at, OUT if kind == OUT_BEGIN else kind, index, shift), kind == OUT_BEGIN)
             for at, kind, index, shift in it.plan() if at == step]
    return [(c, begin) for c, begin in found if c.graph.live]


def chunks_before(it, step):
    return chunks(it, step - 1) if step else chunks(it.before(), it.before().layer.heads - 1)


def due(count):
    return not isinstance(count, int) or count > 0


def over_graphs(eng, iteration):
    for j in range(FIRST_J, PEEL):
        iteration(iteration_of(j))
    for layer in LAYERS:
        last = layer.first + GRAPHS
        with eng.Fori((layer.first + PEEL) // 2, (last - PEEL) // 2) as i:
            iteration(Iteration(i, 0, layer))
            iteration(Iteration(i, 1, layer))
        for j in range(last - PEEL, min(last + PEEL - 1, LAST_J) + 1):
            iteration(iteration_of(j))


def build(nc, x, adj, gamma, beta, wqkv0, wo0, bo0, wq1, wk1, wv1, wo1, bo1, out):
    with ExitStack() as ctx:
        def sb(name, shape, dtype=F32):
            return ctx.enter_context(nc.sbuf_tensor(name, shape, dtype))

        def psum(name):
            return ctx.enter_context(nc.psum_tensor(name, [P, 512], F32))

        def sem(name):
            return ctx.enter_context(nc.semaphore(name))

        score_ps = [psum(f"score_ps{b}") for b in range(2)]
        probT_ps = [psum(f"probT_ps{b}") for b in range(2)]
        value_ps = [psum(f"value_ps{b}") for b in range(2)]
        work_ps = [psum(f"work_ps{b}") for b in range(2)]

        ident = sb("ident", [P, P])
        eps_t = sb("eps_t", [P, NT])
        minus_half = sb("minus_half", [P, NT])
        minus_one = sb("minus_one", [P, NT])
        gamma_b = sb("gamma_b", [P, EMB])
        beta_b = sb("beta_b", [P, EMB])
        mid = sb("mid", [P, GRAPHS, NT, EMB])
        x_in = [sb(f"x_in{b}", [P, NT, EMB]) for b in range(2)]
        x_res = [sb(f"x_res{b}", [P, NT, EMB]) for b in range(2)]
        adj_in = [sb(f"adj_in{b}", [P, NT, NODES], U8) for b in range(2)]
        mask = [sb(f"mask{b}", [P, NT, NODES]) for b in range(2)]
        normed = sb("normed", [P, NT, EMB])
        scaled = sb("scaled", [P, NT, EMB])
        h_in = [sb(f"h_in{b}", [P, NT, EMB]) for b in range(2)]
        hT_hi = [sb(f"hT_hi{b}", [P, ET, NODES], F16) for b in range(2)]
        hT_lo = [sb(f"hT_lo{b}", [P, ET, NODES], F16) for b in range(2)]
        qk_hi = sb("qk_hi", [P, 4, 2 * NODES], F16)
        qk_lo = sb("qk_lo", [P, 4, 2 * NODES], F16)
        qk_stack = [sb(f"qk_stack{b}", [P, 2, 4, 2 * NODES], F16) for b in range(2)]
        k_swap = [sb(f"k_swap{b}", [P, 2, 4, NODES], F16) for b in range(2)]
        v_hi = [sb(f"v_hi{b}", [P, NT, 8, VW], F16) for b in range(2)]
        v_lo = [sb(f"v_lo{b}", [P, NT, 8, HD], F16) for b in range(2)]
        low_max = sb("low_max", [P, 2, NT])
        prob = [sb(f"prob{b}", [P, NT, NODES]) for b in range(2)]
        probT_hi = [sb(f"probT_hi{b}", [P, NT, NODES], F16) for b in range(2)]
        probT_lo = [sb(f"probT_lo{b}", [P, NT, NODES], F16) for b in range(2)]
        inv_sum = sb("inv_sum", [P, 2, NT, 2])
        attn = [sb(f"attn{b}", [P, NT, 8 * HD]) for b in range(2)]
        attnT_hi = sb("attnT_hi", [P, NT, 4, P], F16)
        attnT_lo = sb("attnT_lo", [P, NT, 4, P], F16)
        y = [sb(f"y{b}", [P, NT, EMB]) for b in range(2)]
        y_out = [sb(f"y_out{b}", [P, NT, EMB]) for b in range(2)]

        class Stats:

            def __init__(self, name):
                self.parts = sb(f"{name}_parts", [P, NT, 6])
                self.mv = sb(f"{name}_mv", [P, NT, 2])
                self.vpe = sb(f"{name}_vpe", [P, NT])
                self.rstd = sb(f"{name}_rstd", [P, NT])
                self.mr = sb(f"{name}_mr", [P, NT])
                self.nmr = sb(f"{name}_nmr", [P, NT])

        class Norm:

            def __init__(self, name, stats):
                self.stats = stats
                self.bn_done = sem(f"{name}_bn_done")
                self.mv_done = sem(f"{name}_mv_done")
                self.vpe_done = sem(f"{name}_vpe_done")
                self.rstd_done = sem(f"{name}_rstd_done")
                self.mr_done = sem(f"{name}_mr_done")
                self.nmr_done = sem(f"{name}_nmr_done")

        class Weights:

            def __init__(self, ly):
                self.w_hi = sb(f"w_hi{ly.index}", [P, ET, 3 * ly.inner], F16)
                self.w_lo = sb(f"w_lo{ly.index}", [P, ET, 3 * ly.inner], F16)
                self.wo_hi = sb(f"wo_hi{ly.index}", [P, ly.pairs, EMB], F16)
                self.wo_lo = sb(f"wo_lo{ly.index}", [P, ly.pairs, EMB], F16)
                self.bias = sb(f"bias{ly.index}", [P, EMB])

        x_loaded = [sem(f"x_loaded{b}") for b in range(2)]
        adj_loaded = [sem(f"adj_loaded{b}") for b in range(2)]
        res_loaded = [sem(f"res_loaded{b}") for b in range(2)]
        stored = [sem(f"stored{b}") for b in range(2)]
        first_stacked = [sem(f"first_stacked{half}") for half in range(2)]
        stacked = [[sem(f"stacked{b}_{half}") for half in range(2)] for b in range(2)]
        x_norm = Norm("x", Stats("x_stats"))
        y_norm = Norm("y", Stats("y_stats"))
        x_normed, x_scaled, h_ready = sem("x_normed"), sem("x_scaled"), sem("h_ready")
        res_ready = sem("res_ready")
        mask_raw = sem("mask_raw")
        mask_ready = sem("mask_ready")
        finished = sem("finished")
        work_done, work_hi_done, work_read = sem("work_done"), sem("work_hi_done"), sem("work_read")
        scores_done, masked, probs = sem("scores_done"), sem("masked"), sem("probs")
        probT_done, probT_hi_done, probT_lo_done = sem("probT_done"), sem("probT_hi_done"), sem("probT_lo_done")
        values_done = sem("values_done")
        inv_done, attn_done = sem("inv_done"), sem("attn_done")
        qk_weights_loaded, v_weights_loaded = sem("qk_weights_loaded"), sem("v_weights_loaded")
        out_weights_loaded, weights1_loaded = sem("out_weights_loaded"), sem("weights1_loaded")
        affine_loaded, biases_loaded = sem("affine_loaded"), sem("biases_loaded")
        weights_hi, weights_lo = sem("weights_hi"), sem("weights_lo")
        zeroed, constants = sem("zeroed"), sem("constants")
        sp_passed, pool_passed, dve_passed = sem("sp_passed"), sem("pool_passed"), sem("dve_passed")

        weights = [Weights(ly) for ly in LAYERS]
        w0, w1 = weights

        stage0 = mid[:, 20:26].rearrange("p g t e -> p (g t e)").rearrange("p (c n) -> p c n", c=ET)
        stage_o0 = mid[:, 26:28].rearrange("p g t e -> p (g t) e")
        stage1 = mid[:, 28:31].rearrange("p g t e -> p (g t e)").rearrange("p (c n) -> p c n", c=ET)
        stage_o1 = mid[:, 31:32].rearrange("p g t e -> p (g t) e")

        def of_role(array, ly, k):
            return array[:, :, 0:2 * ly.inner].rearrange("p c (r k n) -> p c r k n", k=2, n=P)[:, :, :, k, :]

        def of_pair(array, p):
            return array[:, :, 2 * P * p:2 * P * (p + 1)]

        def of_values(array, ly):
            return array[:, :, 2 * ly.inner:]

        pieces = [(qk_weights_loaded, 2 * ET * DMA, of_pair(stage0, p), of_pair(w0.w_hi, p), of_pair(w0.w_lo, p))
                  for p in range(LAYER0.pairs)]
        pieces += [(v_weights_loaded, DMA, of_values(stage0, LAYER0), of_values(w0.w_hi, LAYER0),
                    of_values(w0.w_lo, LAYER0)),
                   (out_weights_loaded, DMA, stage_o0, w0.wo_hi[:, :, :], w0.wo_lo[:, :, :]),
                   (weights1_loaded, (2 * ET + 2) * DMA, stage1, w1.w_hi[:, :, :], w1.w_lo[:, :, :]),
                   (weights1_loaded, (2 * ET + 2) * DMA, stage_o1, w1.wo_hi[:, :, :], w1.wo_lo[:, :, :])]
        V_PIECE, OUT_PIECE = LAYER0.pairs, LAYER0.pairs + 1
        split_after = {(-2, 4): pieces[:V_PIECE], (-2, 7): pieces[V_PIECE:OUT_PIECE + 1],
                       (-1, 7): pieces[OUT_PIECE + 1:]}

        def pieces_after(it, step):
            return split_after.get((it.j, step), []) if it.fixed else []

        def normed_inputs(it):
            shifts = {-2: [2, 3], -1: []}.get(it.j, [2]) if it.fixed else [2]
            found = [(Graph(it, t), n == 1) for n, t in enumerate(shifts)]
            return [(g, second) for g, second in found if g.live and g.layer is LAYER0]

        def nodes_of(array, g):
            return array[bass.ds(g.index, 1)].rearrange("g (t p) c -> p (g t) c", p=P)

        def mid_of(g):
            return mid[:, bass.ds(g.index, 1)].rearrange("p g t e -> p (g t) e")

        def in_two(ps):
            return ps[:, :].rearrange("p (c n) -> p c n", c=2)

        def in_four(ps):
            return ps[:, :].rearrange("p (r n) -> p r n", n=P)

        def by_head(ps):
            return ps[:, :].rearrange("p (h d) -> p h d", d=HD)

        def qk_place(g, pair):
            return pair + (LAYER1.pairs * g.par if g.layer is LAYER1 else 0)

        def v_dest(tile, c):
            flat = tile[:, :, :, :].rearrange("p t h d -> p (t h) d")
            return flat[:, 8 * c:8 * c + 8, 0:HD]

        def v_head(ly, tile, kt, head, width):
            flat = tile[:, :, :, :].rearrange("p t h d -> p (t h) d")
            return flat[:, kt * ly.heads + head, 0:width]

        def attnT_dest(tile, c):
            flat = tile[:, :, :, :].rearrange("p t r n -> p (t r) n")
            return flat[:, 4 * c:4 * c + 4, :]

        def attnT_block(ly, tile, t, pair):
            flat = tile[:, :, :, :].rearrange("p t r n -> p (t r) n")
            return flat[:, t * ly.pairs + pair, :]

        X_STATS_STEP, X_MV_STEP, X_NORM_STEPS = 0, 1, (2, 3)
        SECOND_STATS_STEP, SECOND_MV_STEP, SECOND_NORM_STEPS = 3, 4, (7, 7)
        FINISH_STEPS = ((0, 1), (2, 3))

        block = ctx.enter_context(nc.Block())

        @block.sync
        def _(sp):
            by_row = "(c p) n -> p c n"

            def load_input(g):
                if g.after(-2).layer is LAYER0:
                    if due(g.n - 1):
                        sp.wait_ge(x_normed, g.n - 1)
                else:
                    sp.wait_ge(work_done, through(INPUT_T, 0, g.after(-2)))
                if g.layer is LAYER0:
                    src = nodes_of(x, g)
                else:
                    if g.it.fixed and g.index < GRAPHS:
                        sp.wait_ge(stored[g.par], DMA * (g.index // 2 + 1))
                    src = mid_of(g)
                sp.dma_start(x_in[g.par][:, :, :], src).then_inc(x_loaded[g.par], DMA)

            def stack(g, first_pair, end_pair):
                sp.wait_ge(work_read, through(QK, end_pair - 1, g))
                sp.sem_inc(sp_passed, 1)
                if due(g.after(-1).head(0)):
                    sp.wait_ge(scores_done, g.after(-1).head(0))
                    sp.sem_inc(sp_passed, 1)
                for half in range(2):
                    rows, to = slice(HD * half, HD * half + HD), slice(first_pair, end_pair)
                    at = slice(qk_place(g, first_pair), qk_place(g, end_pair))
                    done = stacked[g.par][half] if end_pair == g.layer.pairs else first_stacked[half]
                    both, swap = qk_stack[g.par][:, half, to, :], k_swap[g.par][:, half, to, :]
                    for dst, src in ((both[0:HD], qk_hi[rows, at, :]),
                                     (both[HD:P], qk_lo[rows, at, :]),
                                     (swap[0:HD], qk_lo[rows, at, NODES:2 * NODES]),
                                     (swap[HD:P], qk_hi[rows, at, NODES:2 * NODES])):
                        sp.dma_start(dst, src).then_inc(done, DMA)

            def iteration(it):
                if it.fixed:
                    shifts = [] if it.j < -1 else [3] if it.j < GRAPHS - 1 else [3, 4] if it.j < GRAPHS else [4]
                else:
                    shifts = [3 + it.layer.index]
                for t in shifts:
                    if Graph(it, t).live:
                        load_input(Graph(it, t))
                g = Graph(it, 2)
                if g.live:
                    if due(g.n - 1):
                        sp.wait_ge(mask_raw if g.after(-2).layer is LAYER0 else mask_ready, g.n - 1)
                        sp.sem_inc(sp_passed, 1)
                    sp.dma_start(adj_in[g.par][:, :, :], nodes_of(adj, g)).then_inc(adj_loaded[g.par], DMA)
                g = Graph(it, 0)
                if g.live:
                    if due(g.n - 1):
                        sp.wait_ge(work_read, through(OUT, 0, g.after(-2)))
                    src = nodes_of(x, g) if g.layer is LAYER0 else mid_of(g)
                    sp.dma_start(x_res[g.par][:, :, :], src).then_inc(res_loaded[g.par], DMA)
                projected = [Graph(it, t) for _, kind, index, t in it.plan()
                             if kind == QK and index == Graph(it, t).layer.pairs - 1 and Graph(it, t).live]
                for g in projected[:1]:
                    if g.is_number(0):
                        stack(g, 0, 1)
                        stack(g, 1, g.layer.pairs)
                    else:
                        stack(g, 0, g.layer.pairs)
                g = Graph(it, -2)
                if g.live:
                    if g.is_number(0):
                        sp.wait_ge(weights_lo, len(pieces))
                    sp.wait_ge(finished, g.n + 1)
                    dst = mid_of(g) if g.layer is LAYER0 else nodes_of(out, g)
                    sp.dma_start(dst, y_out[g.par][:, :, :]).then_inc(stored[g.par], DMA)
                for g in projected[1:]:
                    stack(g, 0, g.layer.pairs)
                if it.fixed and it.j == GRAPHS + PEEL - 1:
                    for b in range(2):
                        sp.wait_ge(stored[b], DMA * GRAPHS // 2)

            load_input(Graph(iteration_of(0), 0))
            for k in range(2):
                rows = wqkv0[:, k * LAYER0.inner:(k + 1) * LAYER0.inner]
                for e in range(ET):
                    sp.dma_start(of_role(stage0, LAYER0, k)[:, e],
                                 rows[e * P:(e + 1) * P].rearrange("p (r n) -> p r n", n=P)).then_inc(
                                     qk_weights_loaded, DMA)
            for tile, row in ((gamma_b, gamma), (beta_b, beta)):
                sp.dma_start(tile[:, :], row.partition_broadcast(P)).then_inc(affine_loaded, DMA)
            load_input(Graph(iteration_of(0), 1))
            sp.dma_start(of_values(stage0, LAYER0), wqkv0[:, 2 * LAYER0.inner:].rearrange(by_row, p=P)).then_inc(
                v_weights_loaded, DMA)
            sp.dma_start(stage_o0, wo0.rearrange(by_row, p=P)).then_inc(out_weights_loaded, DMA)
            for tile, row in ((w0.bias, bo0), (w1.bias, bo1)):
                sp.dma_start(tile[:, :], row.partition_broadcast(P)).then_inc(biases_loaded, DMA)
            for k, w in enumerate((wq1, wk1)):
                for e in range(ET):
                    sp.dma_start(of_role(stage1, LAYER1, k)[:, e],
                                 w[e * P:(e + 1) * P].rearrange("p (r n) -> p r n", n=P)).then_inc(weights1_loaded, DMA)
            sp.dma_start(of_values(stage1, LAYER1), wv1.rearrange(by_row, p=P)).then_inc(weights1_loaded, DMA)
            sp.dma_start(stage_o1, wo1.rearrange(by_row, p=P)).then_inc(weights1_loaded, DMA)
            over_graphs(sp, iteration)
            for b in range(2):
                sp.wait_ge(stored[b], DMA * GRAPHS)

        @block.gpsimd
        def _(pool):
            nc.gpsimd.memset(ident[:, :], 0.0).then_inc(zeroed, 1)
            pool.wait_ge(zeroed, 1)
            nc.gpsimd.affine_select(out=ident[:, :], in_=ident[:, :], compare_op=ALU.not_equal, fill=1.0, base=0,
                                    pattern=[[-1, P]], channel_multiplier=1).then_inc(constants, 1)
            nc.gpsimd.memset(eps_t[:, :], EPS).then_inc(constants, 1)
            nc.gpsimd.memset(minus_half[:, :], -0.5).then_inc(constants, 1)
            nc.gpsimd.memset(minus_one[:, :], -1.0).then_inc(constants, 1)
            for b in range(2):
                nc.gpsimd.memset(v_hi[b][:, :, :, HD:VW], 1.0).then_inc(constants, 1)
            pool.wait_ge(constants, 6)

            def normaliser(norm, count):
                st = norm.stats
                nc.gpsimd.tensor_tensor(st.vpe[:, :], st.mv[:, :, 1], eps_t[:, :], ALU.add).then_inc(norm.vpe_done, 1)
                pool.wait_ge(norm.vpe_done, count)
                nc.gpsimd.tensor_tensor(st.rstd[:, :], st.vpe[:, :], minus_half[:, :],
                                        ALU.pow).then_inc(norm.rstd_done, 1)
                pool.wait_ge(norm.rstd_done, count)
                nc.gpsimd.tensor_tensor(st.mr[:, :], st.mv[:, :, 0], st.rstd[:, :],
                                        ALU.mult).then_inc(norm.mr_done, 1)
                pool.wait_ge(norm.mr_done, count)
                nc.gpsimd.tensor_tensor(st.nmr[:, :], st.mr[:, :], minus_one[:, :],
                                        ALU.mult).then_inc(norm.nmr_done, 1)

            def wide(row):
                return row[:, :].unsqueeze(1).broadcast_to([P, NT, EMB])

            def affine(g):
                if g.is_number(0):
                    pool.wait_ge(affine_loaded, 2 * DMA)
                pool.wait_ge(x_normed, g.n + 1)
                nc.gpsimd.tensor_tensor(scaled[:, :, :], normed[:, :, :], wide(gamma_b),
                                        ALU.mult).then_inc(x_scaled, 1)
                pool.wait_ge(x_scaled, g.n + 1)
                if due(g.n - 1):
                    pool.wait_ge(work_done, through(INPUT_T, 0, g.after(-2)))
                nc.gpsimd.tensor_tensor(h_in[g.par][:, :, :], scaled[:, :, :], wide(beta_b),
                                        ALU.add).then_inc(h_ready, 1)

            def masks(it):
                g = Graph(it, 1)
                if g.live:
                    pool.wait_ge(adj_loaded[g.par], DMA * (g.turn + 1))
                    if due(g.after(-1).head(0)):
                        pool.wait_ge(masked, g.after(-1).head(0))
                    pool.sem_inc(pool_passed, 1)
                    nc.gpsimd.tensor_scalar(mask[g.par][:, :, :], adj_in[g.par][:, :, :], BIG, BIG,
                                            ALU.mult, ALU.subtract).then_inc(
                                                mask_raw if g.layer is LAYER0 else mask_ready, 1)
                    if g.layer is LAYER0:
                        pool.wait_ge(mask_raw, g.n + 1)
                        pool.sem_inc(pool_passed, 1)
                        nc.gpsimd.affine_select(out=mask[g.par][:, :, :], in_=mask[g.par][:, :, :],
                                                compare_op=ALU.not_equal, fill=0.0, base=0,
                                                pattern=[[P, NT], [-1, NODES]],
                                                channel_multiplier=1).then_inc(mask_ready, 1)

            def iteration(it):
                g = Graph(it, -2)
                if g.live:
                    pool.wait_ge(y_norm.mv_done, g.n + 1)
                    if due(g.n):
                        pool.wait_ge(finished, g.n)
                    normaliser(y_norm, g.n + 1)
                to_norm = normed_inputs(it)
                for g, second in to_norm:
                    if second:
                        affine(g.after(-1))
                    pool.wait_ge(x_norm.mv_done, g.n + 1)
                    if due(g.n):
                        pool.wait_ge(x_normed, g.n)
                    normaliser(x_norm, g.n + 1)
                masks(it)
                for g, _ in to_norm[-1:]:
                    affine(g)
                g = Graph(it, 0)
                if g.live:
                    if g.is_number(0):
                        pool.wait_ge(biases_loaded, 2 * DMA)
                    pool.wait_ge(res_loaded[g.par], DMA * (g.turn + 1))
                    nc.gpsimd.tensor_tensor(x_res[g.par][:, :, :], x_res[g.par][:, :, :],
                                            wide(weights[g.layer.index].bias), ALU.add).then_inc(res_ready, 1)

            over_graphs(pool, iteration)

        @block.scalar
        def _(act):
            def high_part(c):
                g, ps = c.graph, work_ps[c.bank]
                act.wait_ge(work_done, c.count + 1)
                if c.kind == INPUT_T:
                    e = nc.scalar.activation(hT_hi[g.par][:, :, :], in_two(ps), ACT.Copy)
                elif c.kind == QK:
                    old = g.after(-1 if g.layer is LAYER0 or g.is_number(GRAPHS) else -2)
                    if c.index == 0 and due(old.turn + 1):
                        for half in range(2):
                            act.wait_ge(stacked[old.par][half], 4 * DMA * (old.turn + 1))
                    e = nc.scalar.activation(qk_hi[:, qk_place(g, c.index), :], ps[:, :], ACT.Copy, scale=1 / WSCALE)
                elif c.kind == V:
                    if due(g.after(-1).head(0)):
                        act.wait_ge(values_done, g.after(-1).head(0))
                    e = nc.scalar.activation(v_dest(v_hi[g.par], c.index), by_head(ps), ACT.Copy,
                                             scale=1 / WSCALE)
                else:
                    e = nc.scalar.activation(attnT_dest(attnT_hi, c.index), in_four(ps), ACT.Copy)
                e.then_inc(work_hi_done, 1)

            def apply_norm(norm, dst, src, t):
                return nc.scalar.activation(dst[:, t, :], src[:, t, :], ACT.Identity,
                                            bias=norm.stats.nmr[:, t:t + 1], scale=norm.stats.rstd[:, t:t + 1])

            def iteration(it):
                g, last, older = (Graph(it, t) for t in (0, -1, -2))
                for h in range(it.layer.heads):
                    b = h % 2
                    for c in chunks_before(it, h):
                        if c.kind != OUT:
                            high_part(c)
                    gt = g if h >= 1 else last
                    if gt.live:
                        n = g.head(h) - 1
                        act.wait_ge(probT_done, n + 1)
                        if due(n - 1):
                            act.wait_ge(values_done, n - 1)
                        nc.scalar.activation(probT_hi[1 - b][:, :, :], in_two(probT_ps[1 - b]),
                                             ACT.Copy).then_inc(probT_hi_done, 1)
                    if g.live:
                        n = g.head(h)
                        act.wait_ge(masked, n + 1)
                        if due(n - 1):
                            act.wait_ge(probT_done, n - 1)
                        for qt in range(NT):
                            e = nc.scalar.activation(prob[b][:, qt, :],
                                                     score_ps[b][:, qt * NODES:(qt + 1) * NODES],
                                                     ACT.Exp, bias=low_max[:, b, qt:qt + 1], scale=-1.0)
                        e.then_inc(probs, 1)
                    if older.live:
                        finish = FINISH_STEPS[it.layer.index]
                        if h == finish[0]:
                            act.wait_ge(y_norm.nmr_done, older.n + 1)
                            if due(older.turn):
                                act.wait_ge(stored[older.par], DMA * older.turn)
                        for t in range(NT):
                            if h == finish[t]:
                                e = apply_norm(y_norm, y_out[older.par], y[older.par], t)
                        if h == finish[-1]:
                            e.then_inc(finished, 1)
                    for ahead, second in normed_inputs(it):
                        steps = SECOND_NORM_STEPS if second else X_NORM_STEPS
                        if h == steps[0]:
                            act.wait_ge(x_norm.nmr_done, ahead.n + 1)
                            if due(ahead.n):
                                act.wait_ge(x_scaled, ahead.n)
                        for t in range(NT):
                            if h == steps[t]:
                                e = apply_norm(x_norm, normed, x_in[ahead.par], t)
                        if h == steps[-1]:
                            e.then_inc(x_normed, 1)
                    for loaded, count, stage, hi, _ in pieces_after(it, h):
                        act.wait_ge(loaded, count)
                        nc.scalar.activation(hi, stage, ACT.Copy, scale=WSCALE).then_inc(weights_hi, 1)

            over_graphs(act, iteration)

        @block.vector
        def _(dve):
            def partial_statistics(norm, tile):
                for t in range(NT):
                    e = nc.vector.bn_stats(norm.stats.parts[:, t, :], tile[:, t, :])
                e.then_inc(norm.bn_done, 1)

            def mean_and_variance(norm, count):
                st = norm.stats
                if due(count - 1):
                    dve.wait_ge(norm.nmr_done, count - 1)
                dve.wait_ge(norm.bn_done, count)
                dve.sem_inc(dve_passed, 1)
                for t in range(NT):
                    e = nc.vector.bn_aggr(st.mv[:, t, :], st.parts[:, t, :])
                e.then_inc(norm.mv_done, 1)

            def low_part(c):
                g, ps = c.graph, work_ps[c.bank]
                dve.wait_ge(work_hi_done, c.split + 1)
                if c.kind == INPUT_T:
                    e = nc.vector.tensor_tensor(hT_lo[g.par][:, :, :], in_two(ps), hT_hi[g.par][:, :, :], ALU.subtract)
                elif c.kind == QK:
                    at = qk_place(g, c.index)
                    e = nc.vector.scalar_tensor_tensor(out=qk_lo[:, at, :], in0=ps[:, :], scalar=1 / WSCALE,
                                                       in1=qk_hi[:, at, :], op0=ALU.mult, op1=ALU.subtract)
                elif c.kind == V:
                    flat = v_lo[g.par][:, :, :, :].rearrange("p t h d -> p (t h) d")
                    e = nc.vector.scalar_tensor_tensor(out=flat[:, 8 * c.index:8 * c.index + 8, :], in0=by_head(ps),
                                                       scalar=1 / WSCALE, in1=v_dest(v_hi[g.par], c.index),
                                                       op0=ALU.mult, op1=ALU.subtract)
                else:
                    e = nc.vector.tensor_tensor(attnT_dest(attnT_lo, c.index), in_four(ps),
                                                attnT_dest(attnT_hi, c.index), ALU.subtract)
                e.then_inc(work_read, 1)

            def residual(c):
                g = c.graph
                dve.wait_ge(work_done, c.count + 1)
                dve.wait_ge(res_ready, g.n + 1)
                if due(g.n - 1):
                    dve.wait_ge(finished, g.n - 1)
                nc.vector.scalar_tensor_tensor(out=y[g.par][:, :, :], in0=in_two(work_ps[c.bank]),
                                               scalar=1 / WSCALE, in1=x_res[g.par][:, :, :],
                                               op0=ALU.mult, op1=ALU.add).then_inc(work_read, 1)
                dve.wait_ge(work_read, c.count + 1)
                partial_statistics(y_norm, y[g.par])

            def iteration(it):
                g, nxt, last = (Graph(it, t) for t in (0, 1, -1))
                for h in range(it.layer.heads):
                    b = h % 2
                    before = chunks_before(it, h)
                    for c in before:
                        if c.kind == OUT:
                            residual(c)
                        else:
                            low_part(c)
                    gt = g if h >= 1 else last
                    if gt.live:
                        n = g.head(h) - 1
                        dve.wait_ge(probT_hi_done, n + 1)
                        nc.vector.tensor_tensor(probT_lo[1 - b][:, :, :], in_two(probT_ps[1 - b]),
                                                probT_hi[1 - b][:, :, :], ALU.subtract).then_inc(probT_lo_done, 1)
                    for c in before:
                        if c.kind == OUT:
                            mean_and_variance(y_norm, c.graph.n + 1)
                    for ahead, second in normed_inputs(it):
                        if h == (SECOND_MV_STEP if second else X_MV_STEP):
                            mean_and_variance(x_norm, ahead.n + 1)
                    gv, pair = (g, (h - 2) // 2) if h >= 2 else (last, last.layer.pairs - 1)
                    pair_complete = h % 2 == 1 and gv.live
                    if pair_complete:
                        k = gv.pair(pair)
                        done = value_ps[pair % 2][:, 0:2 * NT * VW].rearrange("p (t h d) -> p t h d", t=NT, h=2)
                        dve.wait_ge(values_done, 2 * k + 2)
                        nc.vector.reciprocal(inv_sum[:, pair % 2], done[:, :, :, HD]).then_inc(inv_done, 1)
                    gs, hs = (g, h + 1) if h + 1 < it.layer.heads else (nxt, 0)
                    if gs.live:
                        if hs == 0:
                            dve.wait_ge(mask_ready, gs.n + 1)
                        dve.wait_ge(scores_done, g.head(h) + 2)
                        dve.sem_inc(dve_passed, 1)
                        for qt in range(NT):
                            sc = score_ps[1 - b][:, qt * NODES:(qt + 1) * NODES]
                            e = nc.vector.tensor_tensor_reduce(sc, sc, mask[gs.par][:, qt, :], -SCALE, BIG,
                                                               ALU.add, ALU.min, low_max[:, 1 - b, qt:qt + 1])
                        e.then_inc(masked, 1)
                    if pair_complete:
                        dve.wait_ge(inv_done, k + 1)
                        if due(gv.n - 1) and pair == 0:
                            old = gv.after(-2)
                            dve.wait_ge(work_done, through(ATTN_T, old.layer.pairs // 2 - 1, old))
                        dst = attn[gv.par][:, :, pair * P:(pair + 1) * P].rearrange("p t (h d) -> p t h d", h=2)
                        nc.vector.tensor_tensor(dst, done[:, :, :, 0:HD],
                                                inv_sum[:, pair % 2].unsqueeze(3).broadcast_to([P, NT, 2, HD]),
                                                ALU.mult).then_inc(attn_done, 1)
                    for ahead, second in normed_inputs(it):
                        if h == (SECOND_STATS_STEP if second else X_STATS_STEP):
                            if second:
                                dve.wait_ge(x_norm.mv_done, ahead.n)
                            dve.wait_ge(x_loaded[ahead.par], DMA * (ahead.turn + 1))
                            partial_statistics(x_norm, x_in[ahead.par])
                    for _, _, stage, hi, lo in pieces_after(it, h):
                        dve.wait_ge(weights_hi, [piece[2] is stage for piece in pieces].index(True) + 1)
                        nc.vector.scalar_tensor_tensor(out=lo, in0=stage, scalar=WSCALE, in1=hi,
                                                       op0=ALU.mult, op1=ALU.subtract).then_inc(weights_lo, 1)

            over_graphs(dve, iteration)

        @block.tensor
        def _(pe):
            def split_product(dst, terms):
                mms = [(a, b) for lhi, llo, rhi, rlo in terms for a, b in ((lhi, rhi), (lhi, rlo), (llo, rhi))]
                for n, (a, b) in enumerate(mms):
                    m = nc.tensor.matmul(dst, a, b, start=n == 0, stop=n == len(mms) - 1)
                return m

            def input_transposed(c):
                g, ps = c.graph, work_ps[c.bank]
                if g.layer is LAYER0:
                    src = h_in[g.par]
                    pe.wait_ge(h_ready, g.n + 1)
                else:
                    src = x_in[g.par]
                    pe.wait_ge(x_loaded[g.par], DMA * (g.turn + 1))
                for t in range(NT):
                    for e in range(ET):
                        at = e * NODES + t * P
                        m = nc.tensor.transpose(ps[:, at:at + P], src[:, t, e * P:(e + 1) * P], ident[:, :])
                return m

            def queries_keys(c):
                w = weights[c.graph.layer.index]
                for k in range(2):
                    at = (2 * c.index + k) * P
                    m = split_product(work_ps[c.bank][:, k * NODES:(k + 1) * NODES],
                                      [(w.w_hi[:, e, at:at + P], w.w_lo[:, e, at:at + P],
                                        hT_hi[c.graph.par][:, e, :], hT_lo[c.graph.par][:, e, :]) for e in range(ET)])
                return m

            def values_projected(c):
                ly, w = c.graph.layer, weights[c.graph.layer.index]
                tiles, par = [c.index] if ly is LAYER0 else range(NT), c.graph.par
                for k, t in enumerate(tiles):
                    m = split_product(work_ps[c.bank][:, k * ly.inner:(k + 1) * ly.inner],
                                      [(hT_hi[par][:, e, t * P:(t + 1) * P], hT_lo[par][:, e, t * P:(t + 1) * P],
                                        w.w_hi[:, e, 2 * ly.inner:], w.w_lo[:, e, 2 * ly.inner:])
                                       for e in range(ET)])
                return m

            def attention_transposed(c):
                ly = c.graph.layer
                if c.index == 0:
                    pe.wait_ge(attn_done, c.graph.pair(ly.pairs))
                for k in range(4):
                    t, pair = divmod(4 * c.index + k, ly.pairs)
                    m = nc.tensor.transpose(work_ps[c.bank][:, k * P:(k + 1) * P],
                                            attn[c.graph.par][:, t, pair * P:(pair + 1) * P], ident[:, :])
                return m

            def output_product(c, begin):
                ly, w = c.graph.layer, weights[c.graph.layer.index]
                begun = any(kind == OUT_BEGIN for _, kind, _, _ in c.graph.it.plan())
                for t in range(NT):
                    if begun and begin != (t == 0):
                        continue
                    pe.wait_ge(work_read, through(ATTN_T, t * (ly.pairs // 2 - 1), c.graph))
                    m = split_product(work_ps[c.bank][:, t * EMB:(t + 1) * EMB],
                                      [(attnT_block(ly, attnT_hi, t, p), attnT_block(ly, attnT_lo, t, p),
                                        w.wo_hi[:, p, :], w.wo_lo[:, p, :]) for p in range(ly.pairs)])
                return m

            def work(c, begin):
                if due(c.count - 1):
                    pe.wait_ge(work_read, c.count - 1)
                if c.graph.is_number(0) and c.kind in (QK, V, OUT):
                    pe.wait_ge(weights_lo, {QK: c.index, V: V_PIECE, OUT: OUT_PIECE}[c.kind] + 1)
                if c.graph.is_number(GRAPHS) and c.kind == QK:
                    pe.wait_ge(weights_lo, len(pieces))
                if c.kind == INPUT_T:
                    m = input_transposed(c)
                elif c.kind == QK:
                    if c.index == 0:
                        pe.wait_ge(work_read, through(INPUT_T, 0, c.graph))
                    m = queries_keys(c)
                elif c.kind == V:
                    m = values_projected(c)
                elif c.kind == ATTN_T:
                    m = attention_transposed(c)
                else:
                    m = output_product(c, begin)
                if not begin:
                    m.then_inc(work_done, 1)

            def scores(g, h):
                n = g.head(h)
                if g.is_number(0) and h < 2:
                    pe.wait_ge(first_stacked[h], 4 * DMA)
                if h < 2 and not g.is_number(0) or g.is_number(0) and 2 <= h < 4:
                    pe.wait_ge(stacked[g.par][h % 2], 4 * DMA * (g.turn + 1))
                if due(n - 1):
                    pe.wait_ge(probs, n - 1)
                for qt in range(NT):
                    dst = score_ps[h % 2][:, qt * NODES:(qt + 1) * NODES]
                    stack, swap = qk_stack[g.par][:, h % 2, h // 2, :], k_swap[g.par][:, h % 2, h // 2, :]
                    q = stack[:, qt * P:(qt + 1) * P]
                    nc.tensor.matmul(dst, q, stack[:, NODES:], start=True, stop=False)
                    m = nc.tensor.matmul(dst, q, swap, start=False, stop=True)
                m.then_inc(scores_done, 1)

            def transpose_probs(g, h):
                n, b = g.head(h), h % 2
                pe.wait_ge(probs, n + 1)
                if due(n - 1):
                    pe.wait_ge(probT_lo_done, n - 1)
                for qt in range(NT):
                    for kt in range(NT):
                        at = kt * NODES + qt * P
                        m = nc.tensor.transpose(probT_ps[b][:, at:at + P], prob[b][:, qt, kt * P:(kt + 1) * P],
                                                ident[:, :])
                m.then_inc(probT_done, 1)

            def values(g, h):
                ly, n, b, pair = g.layer, g.head(h), h % 2, h // 2
                pe.wait_ge(probT_lo_done, n + 1)
                if h % 2 == 0:
                    k = g.pair(pair)
                    if due(k - 1):
                        pe.wait_ge(attn_done, k - 1)
                for qt in range(NT):
                    at = (qt * 2 + h % 2) * VW
                    dst = value_ps[pair % 2][:, at:at + VW]
                    for kt in range(NT):
                        p_hi = probT_hi[b][:, kt, qt * P:(qt + 1) * P]
                        p_lo = probT_lo[b][:, kt, qt * P:(qt + 1) * P]
                        nc.tensor.matmul(dst, p_hi, v_head(ly, v_hi[g.par], kt, h, VW), start=kt == 0, stop=False)
                        nc.tensor.matmul(dst[:, 0:HD], p_hi, v_head(ly, v_lo[g.par], kt, h, HD),
                                         start=False, stop=False)
                        m = nc.tensor.matmul(dst, p_lo, v_head(ly, v_hi[g.par], kt, h, VW),
                                             start=False, stop=kt == NT - 1)
                m.then_inc(values_done, 1)

            def iteration(it):
                g, nxt, last = (Graph(it, t) for t in (0, 1, -1))
                for h in range(it.layer.heads):
                    gt, ht = (g, h - 1) if h >= 1 else (last, last.layer.heads - 1)
                    if gt.live:
                        transpose_probs(gt, ht)
                    gs, hs = (g, h + 1) if h + 1 < it.layer.heads else (nxt, 0)
                    if gs.live:
                        scores(gs, hs)
                    gv, hv = (g, h - 2) if h >= 2 else (last, last.layer.heads - 2 + h)
                    if gv.live:
                        values(gv, hv)
                    for c, begin in chunks_and_begins(it, h):
                        work(c, begin)

            pe.wait_ge(constants, 6)
            over_graphs(pe, iteration)


def kernel(x, adj, L0_gnn_gamma, L0_gnn_beta, L0_gnn_w_qkv, L0_gnn_w_out, L0_gnn_b_out,
           L1_gnn_Wq, L1_gnn_Wk, L1_gnn_Wv, L1_gnn_Wo, L1_gnn_bo):
    import numpy as np
    import concourse.bacc as bacc
    from concourse.bass_utils import run_bass_kernel_spmd

    given = [("x", x), ("adj", adj), ("gamma", L0_gnn_gamma), ("beta", L0_gnn_beta),
             ("wqkv0", np.asarray(L0_gnn_w_qkv).T), ("wo0", np.asarray(L0_gnn_w_out).T), ("bo0", L0_gnn_b_out),
             ("wq1", L1_gnn_Wq), ("wk1", L1_gnn_Wk), ("wv1", L1_gnn_Wv), ("wo1", L1_gnn_Wo), ("bo1", L1_gnn_bo)]
    nc = bacc.Bacc("TRN2", target_bir_lowering=False, num_devices=1)
    arrays, args = {}, []
    for name, a in given:
        a = np.ascontiguousarray(a)
        arrays[f"in_{name}"] = a
        args.append(nc.dram_tensor(f"in_{name}", a.shape, mybir.dt.from_np(a.dtype), kind="ExternalInput").ap())
    out = nc.dram_tensor("out", (GRAPHS, NODES, EMB), F32, kind="ExternalOutput").ap()
    build(nc, *args, out)
    got = run_bass_kernel_spmd(nc, [arrays], core_ids=[0])
    return got.results[0]["out"]
```
